# Optimizing a Trainium2 kernel written in Bass

```python
import numpy as np
import jax
import jax.numpy as jnp

def _softmax(x, axis=-1):
    return jax.nn.softmax(x, axis=axis)

def _gelu(x):
    return jax.nn.gelu(x, approximate=True)

def _silu(x):
    return jax.nn.silu(x)

def _sigmoid(x):
    return jax.nn.sigmoid(x)

def _layernorm(x, axis=-1, eps=1e-05):
    m = jnp.mean(x, axis=axis, keepdims=True)
    v = jnp.var(x, axis=axis, keepdims=True)
    return (x - m) / jnp.sqrt(v + eps)

def _scatter_add(tgt, idx, src, axis=0):
    return tgt.at[idx].add(src)

def _segment_sum(src, seg, n):
    return jax.ops.segment_sum(src, seg, n)
kernel_name = 'mk_xattn_ffn_d1_seqx_r4_a8d2b6'

def setup_inputs(seed: int=0):
    np.random.seed(seed)
    _w = jnp.asarray

    def _rec_inputs():
        import jax
        import jax.numpy as jnp
        _rk = jax.random.key(seed)
        x = -0.0002928 + 1 * jax.random.normal(jax.random.fold_in(_rk, 1), (16, 256, 256), jnp.float32)
        _lenS = 256 - jax.random.randint(jax.random.fold_in(_rk, 7), (16,), 0, max(1, 256 // 4) + 1, jnp.int32)
        _lenS2 = 77 - jax.random.randint(jax.random.fold_in(_rk, 8), (16,), 0, max(1, 77 // 4) + 1, jnp.int32)
        _ctx_1024P = jax.random.normal(jax.random.fold_in(_rk, 11), (16, 16, 256), jnp.float32)
        _ctx_1024c = jax.random.dirichlet(jax.random.fold_in(_rk, 511), 0.3 * jnp.ones((16,), jnp.float32), (16, 77))
        _ctx_1024t = jnp.einsum('bsk,bkd->bsd', _ctx_1024c, _ctx_1024P)
        _ctx_1024t = _ctx_1024t * jax.lax.rsqrt(jnp.mean(jnp.square(_ctx_1024t)) + 1e-12) * 0.953939
        ctx_1024 = -1.39393e-06 + 0.999914 * (_ctx_1024t + 0.3 * jax.random.normal(jax.random.fold_in(_rk, 611), (16, 77, 256), jnp.float32))
        return (x, ctx_1024)
    x, ctx_1024 = _rec_inputs()

    def _L0_xattn_setup():
        import jax, jax.numpy as jnp
        import numpy as np
        D_MODEL = 256
        H = 16
        D_K = D_MODEL // H
        key = jax.random.key(seed)
        ks = jax.random.split(key, 11)
        B, S = (2, 512)
        scale = 1.0 / np.sqrt(D_MODEL)
        inp = {'q': jax.random.normal(ks[0], (B, S, D_MODEL), jnp.float32), 'k': jax.random.normal(ks[1], (B, S, D_MODEL), jnp.float32), 'v': jax.random.normal(ks[2], (B, S, D_MODEL), jnp.float32), 'w_q': jax.random.normal(ks[3], (D_MODEL, D_MODEL), jnp.float32) * scale, 'b_q': jnp.zeros((D_MODEL,), jnp.float32), 'w_k': jax.random.normal(ks[4], (D_MODEL, D_MODEL), jnp.float32) * scale, 'b_k': jnp.zeros((D_MODEL,), jnp.float32), 'w_v': jax.random.normal(ks[5], (D_MODEL, D_MODEL), jnp.float32) * scale, 'b_v': jnp.zeros((D_MODEL,), jnp.float32), 'w_o': jax.random.normal(ks[6], (D_MODEL, D_MODEL), jnp.float32) * scale, 'b_o': jnp.zeros((D_MODEL,), jnp.float32)}
        return inp
    _L0_xattn_all = _L0_xattn_setup()
    _L0_xattn_in = {k: v for k, v in _L0_xattn_all.items() if k in ('w_q', 'b_q', 'w_k', 'b_k', 'w_v', 'b_v', 'w_o', 'b_o')}
    del _L0_xattn_all

    def _L0_ffn_setup():
        import jax, jax.numpy as jnp
        import numpy as np
        NUM_EXPERTS = 8
        TOP_K = 2
        key = jax.random.key(seed)
        k1, k2, k3, k4, k5 = jax.random.split(key, 5)
        B, S, D, F = (4, 512, 256, 1024)
        return {'hidden_states': jax.random.normal(k1, (B, S, D), dtype=jnp.float32), 'router_w': jax.random.normal(k2, (D, NUM_EXPERTS), dtype=jnp.float32) * 0.02, 'gate_w': jax.random.normal(k3, (NUM_EXPERTS, D, F), dtype=jnp.float32) * 0.02, 'up_w': jax.random.normal(k4, (NUM_EXPERTS, D, F), dtype=jnp.float32) * 0.02, 'down_w': jax.random.normal(k5, (NUM_EXPERTS, F, D), dtype=jnp.float32) * 0.02}
    _L0_ffn_all = _L0_ffn_setup()
    _L0_ffn_in = {k: v for k, v in _L0_ffn_all.items() if k in ('router_w', 'gate_w', 'up_w', 'down_w')}
    del _L0_ffn_all
    return {'x': x, 'ctx_1024': ctx_1024, 'L0_xattn_w_q': _L0_xattn_in['w_q'], 'L0_xattn_b_q': _L0_xattn_in['b_q'], 'L0_xattn_w_k': _L0_xattn_in['w_k'], 'L0_xattn_b_k': _L0_xattn_in['b_k'], 'L0_xattn_w_v': _L0_xattn_in['w_v'], 'L0_xattn_b_v': _L0_xattn_in['b_v'], 'L0_xattn_w_o': _L0_xattn_in['w_o'], 'L0_xattn_b_o': _L0_xattn_in['b_o'], 'L0_ffn_router_w': _L0_ffn_in['router_w'], 'L0_ffn_gate_w': _L0_ffn_in['gate_w'], 'L0_ffn_up_w': _L0_ffn_in['up_w'], 'L0_ffn_down_w': _L0_ffn_in['down_w']}

def reference(x, ctx_1024, L0_xattn_w_q, L0_xattn_b_q, L0_xattn_w_k, L0_xattn_b_k, L0_xattn_w_v, L0_xattn_b_v, L0_xattn_w_o, L0_xattn_b_o, L0_ffn_router_w, L0_ffn_gate_w, L0_ffn_up_w, L0_ffn_down_w):
    import jax
    import jax.numpy as jnp

    def _L0_xattn_ref(q, k, v, w_q, b_q, w_k, b_k, w_v, b_v, w_o, b_o):
        import jax, jax.numpy as jnp
        import numpy as np
        D_MODEL = 256
        H = 16
        D_K = D_MODEL // H
        B, S, _ = q.shape

        def proj(x, w, b):
            y = jnp.einsum('bsd,ed->bse', x, w) + b
            return y.reshape(B, -1, H, D_K).transpose(0, 2, 1, 3)
        qh = proj(q, w_q, b_q)
        kh = proj(k, w_k, b_k)
        vh = proj(v, w_v, b_v)
        scores = jnp.einsum('bhqd,bhkd->bhqk', qh, kh) / jnp.sqrt(jnp.float32(D_K))
        attn = jax.nn.softmax(scores, axis=-1)
        ctx = jnp.einsum('bhqk,bhkd->bhqd', attn, vh)
        ctx = ctx.transpose(0, 2, 1, 3).reshape(B, -1, D_MODEL)
        return jnp.einsum('bsd,ed->bse', ctx, w_o) + b_o

    def _L0_ffn_ref(hidden_states, router_w, gate_w, up_w, down_w):
        import jax, jax.numpy as jnp
        import numpy as np
        NUM_EXPERTS = 8
        TOP_K = 2
        B, S, D = hidden_states.shape
        x = hidden_states.reshape(-1, D)
        T = x.shape[0]
        logits = x @ router_w
        probs = jax.nn.softmax(logits.astype(jnp.float32), axis=-1)
        top_w, top_i = jax.lax.top_k(probs, TOP_K)
        top_w = top_w.astype(x.dtype)
        cw = jnp.zeros((T, NUM_EXPERTS), dtype=x.dtype)
        cw = cw.at[jnp.arange(T)[:, None], top_i].set(top_w)
        out = jnp.zeros_like(x)
        for e in range(NUM_EXPERTS):
            h = jax.nn.silu(x @ gate_w[e]) * (x @ up_w[e])
            out = out + cw[:, e:e + 1] * (h @ down_w[e])
        return out.reshape(B, S, D)
    x = x + _L0_xattn_ref(_layernorm(x, axis=-1), ctx_1024, ctx_1024, L0_xattn_w_q, L0_xattn_b_q, L0_xattn_w_k, L0_xattn_b_k, L0_xattn_w_v, L0_xattn_b_v, L0_xattn_w_o, L0_xattn_b_o)
    x = x + _L0_ffn_ref(_layernorm(x, axis=-1), L0_ffn_router_w, L0_ffn_gate_w, L0_ffn_up_w, L0_ffn_down_w)
    return x

_drawn_inputs = setup_inputs


def setup_inputs(seed=0):
    import zlib

    import numpy as np

    out = dict(_drawn_inputs(seed))
    spreads = {'L0_xattn_b_q': (0.0, 0.391),
     'L0_xattn_b_k': (0.0, 0.8),
     'L0_xattn_b_v': (0.0, 0.1),
     'L0_xattn_b_o': (0.0, 0.1)}
    factors = {'L0_ffn_router_w': 8.0,
     'L0_ffn_gate_w': 7.765,
     'L0_ffn_up_w': 7.673,
     'L0_ffn_down_w': 7.684}
    for name, (base, spread) in spreads.items():
        noise = np.random.default_rng([zlib.crc32(name.encode()), seed]).standard_normal(out[name].shape)
        drawn = base * np.exp(spread * noise) if base else spread * noise
        out[name] = jnp.asarray(drawn.astype(out[name].dtype))
    for name, factor in factors.items():
        out[name] = (out[name] * factor).astype(out[name].dtype)
    return out
```

```python
from contextlib import ExitStack

import numpy as np
import concourse.bass as bass
from concourse import mybir
from concourse.alu_op_type import AluOpType as ALU

F32 = mybir.dt.float32
F16 = mybir.dt.float16
I32 = mybir.dt.int32
U32 = mybir.dt.uint32
ACT = mybir.ActivationFunctionType
AX = mybir.AxisListType

P = 128
B, S, D = 16, 256, 256
KS = 77
H, DK = 16, 16
E, F = 8, 1024
T = B * S
KC = D // P
NT = S // P
FC = F // P
HG = 4
UNITS = NT * H // HG
VW = DK + 1
EPS = 1e-5
WS = 32.0
S_SCALE = 1.0 / (WS * WS * 4.0)
H_DOWN = 1.0 / 256.0
TS = 256
PAD = 2 * TS
REGION = T + PAD
RW = D + E + 1
WCOLS = 3 * KC * F
PIECE = 512
PIECES = WCOLS // PIECE
STEPS = FC // 2
RSQRT_SEED = 0x5F3759DF
LN_STEPS = 2 + 3 + 9 + 1
LOW_ON_ACT = (0, 2, 3, 4, 6, 7)
ROUTE = 3
SCATTER = 2 * NT * 16
LOW = -3.0e38


class At:

    def __init__(self, plus, reg=None, times=0):
        self.plus, self.reg, self.times = plus, reg, times

    def __add__(self, n):
        return At(self.plus + n, self.reg, self.times)

    def __sub__(self, n):
        return self + (-n)

    def value(self, per, k=0):
        n = per * self.plus + k
        return n if self.reg is None else self.reg * (per * self.times) + n


def after(eng, sem, value):
    if not isinstance(value, int) or value > 0:
        eng.wait_ge(sem, value)


def apart(eng, passed):
    eng.sem_inc(passed, 1)


def build(nc, x, ctx_t, w_q, b_q, w_k, b_k, w_v, b_v, w_o, b_o, router_w, gate_w, up_w, down_w, out):
    rows_dram = nc.dram_tensor("expert_rows", (E * REGION, RW), F32, kind="Internal").ap()
    x_tiles = x.rearrange("(b t p) d -> b p t d", t=NT, p=P)
    out_tiles = out[0:T, :].rearrange("(b t p) d -> b p t d", t=NT, p=P)

    with ExitStack() as stack:
        def sb(name, shape, dt=F32):
            return stack.enter_context(nc.sbuf_tensor(name, shape, dt))

        def bank(name):
            return stack.enter_context(nc.psum_tensor(name, [P, 512], F32))

        def sem(name):
            return stack.enter_context(nc.semaphore(name))

        ident = sb("ident", [P, P])
        ident16 = sb("ident16", [P, P], F16)
        before = sb("before", [P, P], F16)
        ones16 = sb("ones16", [P, P], F16)
        minus16 = sb("minus16", [P, P], F16)
        head_mask = sb("head_mask", [P, P // DK], F16)
        expert_i = sb("expert_i", [P, E], I32)
        expert_f = sb("expert_f", [P, E])
        region_i = sb("region_i", [P, E], I32)
        token_i = sb("token_i", [P, NT], I32)
        pads = sb("pads", [P, 2, RW])
        w_stage = sb("w_stage", [P, 4, KC, D])
        w_hi = sb("w_hi", [P, 4, KC, D], F16)
        w_lo = sb("w_lo", [P, 4, KC, D], F16)
        r_stage = sb("r_stage", [P, KC, E])
        r_hi = sb("r_hi", [P, KC, E], F16)
        r_lo = sb("r_lo", [P, KC, E], F16)
        bq = sb("bq", [P, KC])
        bk = sb("bk", [P, KC])
        bq32 = sb("bq32", [P, KC])
        bk32 = sb("bk32", [P, KC])
        bv = sb("bv", [KS, D])
        bv32 = sb("bv32", [KS, D])
        bo = sb("bo", [P, D])
        xin = sb("xin", [P, NT, D])
        xn = sb("xn", [P, NT, D])
        ln_stats = sb("ln_stats", [P, 2 * NT, 6])
        ln_mv = sb("ln_mv", [P, 2 * NT, 2])
        ln_var = sb("ln_var", [P, 2 * NT])
        ln_tmp = sb("ln_tmp", [P, 2 * NT])
        ln_rstd = sb("ln_rstd", [P, 2 * NT])
        ln_bias = sb("ln_bias", [P, 2 * NT])
        xt_hi = sb("xt_hi", [P, KC, S], F16)
        xt_lo = sb("xt_lo", [P, KC, S], F16)
        q_hi = sb("q_hi", [P, 2, KC, S], F16)
        q_lo = sb("q_lo", [P, 2, KC, S], F16)
        cx = sb("cx", [P, KC, KS])
        cx_hi = sb("cx_hi", [P, KC, KS], F16)
        cx_lo = sb("cx_lo", [P, KC, KS], F16)
        k_full = sb("k_full", [P, KC, KS])
        v_full = sb("v_full", [KS, D])
        k_parts = sb("k_parts", [P, 2, KC, KS], F16)
        k_diag = sb("k_diag", [P, 2, 2, KC, P // DK, KS], F16)
        v_parts = sb("v_parts", [KS, 2, 2, H, VW], F16)
        row_max = sb("row_max", [P, 2, HG])
        probs = sb("probs", [P, 2, HG, KS])
        pt_hi = sb("pt_hi", [KS, 2, HG * P], F16)
        pt_lo = sb("pt_lo", [KS, 2, HG * P], F16)
        inv_sum = sb("inv_sum", [P, H])
        att = sb("att", [P, NT, D])
        at_hi = sb("at_hi", [P, KC, S], F16)
        at_lo = sb("at_lo", [P, KC, S], F16)
        xres = sb("xres", [P, NT, D])
        x2 = sb("x2", [P, NT, D])
        x2n = sb("x2n", [P, NT, D])
        x2t = sb("x2t", [P, KC, 2, S], F16)
        rows = sb("rows", [P, 2, NT, RW])
        expl = sb("expl", [P, NT, E])
        top = sb("top", [P, NT, E])
        top_at = sb("top_at", [P, NT, E], U32)
        pick = sb("pick", [P, NT, 2, E])
        both16 = sb("both16", [P, NT, E], F16)
        prob_sum = sb("prob_sum", [P, NT])
        prob_inv = sb("prob_inv", [P, NT])
        weight = sb("weight", [P, NT, E])
        next_row = sb("next_row", [P, E])
        slot = sb("slot", [P, NT, E])
        slot_of = sb("slot_of", [P, NT, 2, E])
        slot_f = sb("slot_f", [P, NT, 2])
        slot_u = sb("slot_u", [P, 2, NT, 2], U32)
        count_f = sb("count_f", [1, E])
        tiles_f = sb("tiles_f", [1, E])
        tiles_i = sb("tiles_i", [1, E], I32)
        tiles_g = sb("tiles_g", [1, E])
        base_a = sb("base_a", [1, E])
        base_b = sb("base_b", [1, E])
        base_i = sb("base_i", [1, E], I32)
        pad_i = sb("pad_i", [1, E], I32)
        rest_f = sb("rest_f", [1, E])
        rest_i = sb("rest_i", [1, E], I32)
        last_i = sb("last_i", [1, E], I32)
        e_stage = sb("e_stage", [P, WCOLS])
        e_hi = sb("e_hi", [P, 2, WCOLS], F16)
        e_lo = sb("e_lo", [P, 2, WCOLS], F16)
        raw = sb("raw", [P, 2, RW])
        tail_in = sb("tail_in", [P, 2, E + 1])
        xg = sb("xg", [P, KC, 2, TS], F16)
        g_act = sb("g_act", [P, 2, 512])
        h_full = sb("h_full", [P, 2, 512])
        h_hi = sb("h_hi", [P, FC, TS], F16)
        h_lo = sb("h_lo", [P, FC, TS], F16)
        w_row = sb("w_row", [P, 2])
        tok_row = sb("tok_row", [P, 2], U32)
        y_sb = sb("y_sb", [P, 2, D])

        banks = [bank(f"bank{n}") for n in range(8)]
        ps_score = [banks[0], banks[1]]
        ps_probs = [banks[2], banks[3]]
        ps_att, ps_a, ps_kv, ps_c = banks[4:8]
        ps_logits = ps_a[:, 0:NT * E].rearrange("p (t e) -> p t e", t=NT)
        ps_ranks = [ps_a[:, (NT + n) * E:(NT + n + 1) * E] for n in range(NT + 1)]
        ps_rank_pair = ps_a[:, NT * E:2 * NT * E].rearrange("p (t e) -> p t e", t=NT)
        ps_x2t = ps_kv[:].bitcast(F16).rearrange("p (c l s) -> p c l s", c=KC, l=2)
        ps_gate = [banks[0], banks[1]]
        ps_up = [banks[2], banks[3]]
        ps_y = [banks[4], banks[5]]
        ps_xt = [banks[6 + c][:, 0:TS].bitcast(F16).rearrange("p (l s) -> p l s", l=2) for c in range(KC)]

        passed = sem("passed")
        w_in = sem("w_in")
        r_in = sem("r_in")
        e_in = sem("e_in")
        w_hi_ready = sem("w_hi_ready")
        w_lo_ready = sem("w_lo_ready")
        bias_ready = sem("bias_ready")
        const_base = sem("const_base")
        const_ready = sem("const_ready")
        x_in = sem("x_in")
        xres_in = sem("xres_in")
        cx_in = sem("cx_in")
        xn_ready = sem("xn_ready")
        xt_turned = sem("xt_turned")
        xt_hi_ready = sem("xt_hi_ready")
        xt_lo_ready = sem("xt_lo_ready")
        q_made = sem("q_made")
        q_hi_ready = sem("q_hi_ready")
        q_lo_ready = sem("q_lo_ready")
        cx_hi_ready = sem("cx_hi_ready")
        cx_lo_ready = sem("cx_lo_ready")
        kv_made = sem("kv_made")
        kv_full = sem("kv_full")
        kv_part = sem("kv_part")
        kd_ready = sem("kd_ready")
        s_made = sem("s_made")
        max_ready = sem("max_ready")
        shifted = sem("shifted")
        exp_ready = sem("exp_ready")
        p_turned = sem("p_turned")
        pt_hi_ready = sem("pt_hi_ready")
        p_rest = sem("p_rest")
        lo_by_act = sem("lo_by_act")
        lo_by_dve = sem("lo_by_dve")
        pv_made = sem("pv_made")
        inv_ready = sem("inv_ready")
        att_ready = sem("att_ready")
        at_turned = sem("at_turned")
        at_hi_ready = sem("at_hi_ready")
        at_lo_ready = sem("at_lo_ready")
        o_made = sem("o_made")
        xb_ready = sem("xb_ready")
        x2_ready = sem("x2_ready")
        ln = sem("ln")
        x2n_ready = sem("x2n_ready")
        x2_turned = sem("x2_turned")
        x2t_ready = sem("x2t_ready")
        logits_made = sem("logits_made")
        route = sem("route")
        route_w = sem("route_w")
        route_s = sem("route_s")
        ones_set = sem("ones_set")
        token_ready = sem("token_ready")
        shift_ready = sem("shift_ready")
        expl_ready = sem("expl_ready")
        both_ready = sem("both_ready")
        ranks_made = sem("ranks_made")
        cw_ready = sem("cw_ready")
        slots_ready = sem("slots_ready")
        row_hi_ready = sem("row_hi_ready")
        row_ready = sem("row_ready")
        scattered = sem("scattered")
        x2_out = sem("x2_out")
        counted = sem("counted")
        tables_ready = sem("tables_ready")
        pad_out = sem("pad_out")
        dummy_out = sem("dummy_out")
        raw_in = sem("raw_in")
        raw_free = sem("raw_free")
        xg_turned = sem("xg_turned")
        xg_act = sem("xg_act")
        xg_vec = sem("xg_vec")
        gu_made = sem("gu_made")
        silu_ready = sem("silu_ready")
        h_ready = sem("h_ready")
        h_hi_ready = sem("h_hi_ready")
        h_lo_ready = sem("h_lo_ready")
        y_made = sem("y_made")
        meta_ready = sem("meta_ready")
        y_ready = sem("y_ready")
        added = sem("added")
        e_hi_ready = sem("e_hi_ready")
        e_lo_ready = sem("e_lo_ready")

        block = stack.enter_context(nc.Block())

        def load_expert(eng, e):
            for m, w in enumerate((gate_w, up_w)):
                eng.dma_start(e_stage[:, m * KC * F:(m + 1) * KC * F].rearrange("p (c f) -> p c f", c=KC),
                              w[bass.ds(e, 1), :, :].rearrange("a (c p) f -> p (a c) f", p=P)).then_inc(e_in, 16)
            eng.dma_start(e_stage[:, 2 * KC * F:].rearrange("p (c d) -> p c d", c=FC),
                          down_w[bass.ds(e, 1), :, :].rearrange("a (c p) d -> p (a c) d", p=P)).then_inc(e_in, 16)

        def batches(eng, body):
            for first in range(4):
                body(*[At(first - stage) if first >= stage else None for stage in range(5)])
            with eng.Fori(0, (B - 4) // 2) as k:
                for odd in range(2):
                    body(*[At(4 + odd - stage, k, 2) for stage in range(5)])
            for first in range(B, B + 4):
                body(*[At(first - stage) if first - stage < B else None for stage in range(5)])

        def ahead(b, a, u):
            at, v = (b, u) if u < UNITS else (a, u - UNITS)
            return (at, v) if at else None

        def low_done(eng, i, u):
            back, v = divmod(u, UNITS)
            on_act = v in LOW_ON_ACT
            done = [w for w in range(v + 1) if (w in LOW_ON_ACT) == on_act]
            per = len(LOW_ON_ACT) if on_act else UNITS - len(LOW_ON_ACT)
            after(eng, lo_by_act if on_act else lo_by_dve, i.value(per, per * back + len(done)))

        def of_act(u):
            return len([w for w in LOW_ON_ACT if w <= u])

        def experts(eng, body):
            with eng.Fori(0, E // 2) as pair:
                for parity in range(2):
                    e = pair * 2 + parity
                    n = eng.value_load(tiles_i[0:1, bass.ds(e, 1)], min_val=2, max_val=T // TS)
                    first = eng.value_load(base_i[0:1, bass.ds(e, 1)], min_val=0, max_val=2 * T // TS + E)
                    body(e, parity, first, n)

        @block.sync
        def _(sp):
            for n, w in enumerate((w_q, w_k, w_v, w_o)):
                sp.dma_start(w_stage[:, n, :, :], w.rearrange("(c p) e -> p c e", p=P)).then_inc(w_in, 16)
            sp.dma_start(xin[:], x_tiles[0]).then_inc(x_in, 16)
            sp.dma_start(cx[:], ctx_t[0].rearrange("(c p) k -> p c k", p=P)).then_inc(cx_in, 16)
            sp.dma_start(bq[:], b_q).then_inc(r_in, 16)
            sp.dma_start(bk[:], b_k).then_inc(r_in, 16)
            sp.dma_start(bv[:], b_v.partition_broadcast(KS)).then_inc(r_in, 16)
            sp.dma_start(bo[:], b_o.partition_broadcast(P)).then_inc(r_in, 16)
            sp.dma_start(r_stage[:], router_w.rearrange("(c p) e -> p c e", p=P)).then_inc(r_in, 16)
            sp.dma_start(xres[:], x_tiles[0]).then_inc(xres_in, 16)
            load_expert(sp, 0)

            def load_a(j):
                after(sp, xn_ready, j.value(NT))
                sp.dma_start(xin[:], x_tiles[bass.ds(j.value(1), 1)].rearrange("a p t d -> p (a t) d")).then_inc(x_in, 16)
                after(sp, cx_lo_ready, j.value(1))
                sp.dma_start(cx[:], ctx_t[bass.ds(j.value(1), 1)].rearrange("a (c p) k -> p (a c) k", p=P)).then_inc(cx_in, 16)

            def store_c(j):
                after(sp, x2_ready, j.value(1, 1))
                sp.dma_start(out_tiles[bass.ds(j.value(1), 1)].rearrange("a p t d -> p (a t) d"), x2[:]).then_inc(x2_out, 16)

            def load_c(j):
                after(sp, x2_ready, j.value(1))
                sp.dma_start(xres[:], x_tiles[bass.ds(j.value(1), 1)].rearrange("a p t d -> p (a t) d")).then_inc(xres_in, 16)

            load_a(At(1))
            load_a(At(2))
            with sp.Fori(0, B - 3) as k:
                load_a(At(3, k, 1))
                store_c(At(0, k, 1))
                load_c(At(1, k, 1))
            for j in range(B - 3, B):
                store_c(At(j))
                if j + 1 < B:
                    load_c(At(j + 1))

            def pad_expert(e):
                at = sp.value_load(pad_i[0:1, bass.ds(e, 1)], min_val=0, max_val=E * REGION - PAD)
                for half in range(PAD // TS):
                    sp.dma_start(rows_dram[bass.ds(at + half * TS, TS), :].rearrange("(s p) w -> p s w", p=P),
                                 pads[:]).then_inc(pad_out, 16)

            sp.wait_ge(tables_ready, 5)
            sp.wait_ge(scattered, SCATTER * B + 16)
            sp.wait_ge(const_ready, 10)
            pad_expert(0)

            def tiles(e, parity, first, n):
                sp.wait_ge(pad_out, e * (16 * PAD // TS) + 16 * PAD // TS)
                apart(sp, passed)
                with sp.Fori(0, n) as j:
                    sp.wait_ge(raw_free, first + j + 1)
                    sp.dma_start(raw[:], rows_dram[bass.ds(e * REGION + j * TS, TS), :].rearrange(
                        "(s p) w -> p s w", p=P)).then_inc(raw_in, 16)
                pad_expert((e + 1) % E)

            experts(sp, tiles)
            total = sp.value_load(base_i[0:1, E - 1:E], min_val=0, max_val=2 * T // TS + E)
            last = sp.value_load(tiles_i[0:1, E - 1:E], min_val=2, max_val=T // TS)
            sp.wait_ge(pad_out, (E + 1) * 16 * PAD // TS)
            sp.wait_ge(raw_free, total + last + 1)
            sp.dma_start(raw[:], rows_dram[0:TS, :].rearrange("(s p) w -> p s w", p=P)).then_inc(raw_in, 16)
            sp.wait_ge(raw_in, (total + last) * 16 + 16)
            sp.wait_ge(x2_out, 16 * B)
            sp.wait_ge(added, (total + last) * 32 + 16)
            apart(sp, passed)

        @block.tensor
        def _(pe):
            def three(dst, a_hi, a_lo, b_hi, b_lo, chunks):
                for c in range(chunks):
                    pe.matmul(dst, a_hi(c), b_hi(c), start=c == 0, stop=False)
                    pe.matmul(dst, a_hi(c), b_lo(c), start=False, stop=False)
                    mm = pe.matmul(dst, a_lo(c), b_hi(c), start=False, stop=c == chunks - 1)
                return mm

            def turn_x(j):
                after(pe, xn_ready, j.value(NT, NT))
                after(pe, q_lo_ready, j.value(KC))
                after(pe, slots_ready, j.value(1, -2))
                for t in range(NT):
                    for c in range(KC):
                        mm = pe.transpose(ps_a[:, c * S + t * P:c * S + (t + 1) * P], xn[:, t, c * P:(c + 1) * P], ident[:])
                mm.then_inc(xt_turned, 1)

            def project_kv(j):
                after(pe, cx_lo_ready, j.value(1, 1))
                after(pe, kv_full, j.value(KC + 1))
                for m in range(KC):
                    three(ps_kv[:, m * KS:(m + 1) * KS],
                          lambda c: w_hi[:, 1, c, m * P:(m + 1) * P], lambda c: w_lo[:, 1, c, m * P:(m + 1) * P],
                          lambda c: cx_hi[:, c, :], lambda c: cx_lo[:, c, :], KC)
                three(ps_kv[0:KS, KC * KS:KC * KS + D], lambda c: cx_hi[:, c, :], lambda c: cx_lo[:, c, :],
                      lambda c: w_hi[:, 2, c, :], lambda c: w_lo[:, 2, c, :], KC).then_inc(kv_made, 1)

            def project_q(j):
                after(pe, xt_lo_ready, j.value(1, 1))
                for m in range(KC):
                    mm = three(ps_a[:, m * S:(m + 1) * S],
                               lambda c: w_hi[:, 0, c, m * P:(m + 1) * P], lambda c: w_lo[:, 0, c, m * P:(m + 1) * P],
                               lambda c: xt_hi[:, c, :], lambda c: xt_lo[:, c, :], KC)
                mm.then_inc(q_made, 1)

            def score(i, par, u):
                t, v = divmod(u, UNITS // NT)
                m, half = divmod(v, 2)
                if u == 0:
                    after(pe, q_lo_ready, i.value(KC, KC))
                    after(pe, kd_ready, i.value(1, 1))
                after(pe, shifted, i.value(UNITS, u - 1))
                keys = [k_diag[:, par, l, m, half * HG:(half + 1) * HG, :].rearrange("p h k -> p (h k)") for l in range(2)]
                three(ps_score[u % 2][:, 0:HG * KS],
                      lambda c: q_hi[:, par, m, t * P:(t + 1) * P], lambda c: q_lo[:, par, m, t * P:(t + 1) * P],
                      lambda c: keys[0], lambda c: keys[1], 1).then_inc(s_made, 1)

            def turn_probs(i, u):
                after(pe, exp_ready, i.value(UNITS, u + 1))
                low_done(pe, i, u - 2)
                for h in range(HG):
                    mm = pe.matmul(ps_probs[u % 2][0:KS, h * P:(h + 1) * P], probs[:, u % 2, h, :], ident[:], is_transpose=True,
                                   start=h == 0, stop=h == HG - 1)
                mm.then_inc(p_turned, 1)

            def take_high(i, u):
                after(pe, pt_hi_ready, i.value(UNITS, u + 1))
                pe.matmul(ps_probs[u % 2][0:KS, :], minus16[0:KS, 0:KS], pt_hi[:, u % 2, :],
                          start=False, stop=True, skip_group_check=True).then_inc(p_rest, 1)

            def weigh_values(i, par, u):
                t, v = divmod(u, UNITS // NT)
                if u == 0:
                    after(pe, kv_part, i.value(4, 4))
                if v == 0:
                    after(pe, att_ready, i.value(NT, t))
                low_done(pe, i, u)
                for g in range(HG):
                    h = v * HG + g
                    mm = three(ps_att[:, h * VW:(h + 1) * VW],
                               lambda c: pt_hi[:, u % 2, g * P:(g + 1) * P], lambda c: pt_lo[:, u % 2, g * P:(g + 1) * P],
                               lambda c: v_parts[:, par, 0, h, :], lambda c: v_parts[:, par, 1, h, :], 1)
                mm.then_inc(pv_made, 1)

            def turn_att(j):
                after(pe, att_ready, j.value(NT, NT))
                after(pe, x2_ready, j.value(1))
                for t in range(NT):
                    for c in range(KC):
                        mm = pe.transpose(ps_c[:, c * S + t * P:c * S + (t + 1) * P], att[:, t, c * P:(c + 1) * P], ident[:])
                mm.then_inc(at_turned, 1)

            def project_o(j):
                after(pe, at_lo_ready, j.value(1, 1))
                for t in range(NT):
                    mm = three(ps_c[:, t * D:(t + 1) * D],
                               lambda c: at_hi[:, c, t * P:(t + 1) * P], lambda c: at_lo[:, c, t * P:(t + 1) * P],
                               lambda c: w_hi[:, 3, c, :], lambda c: w_lo[:, 3, c, :], KC)
                mm.then_inc(o_made, 1)

            def turn_x2(r, par, a):
                after(pe, row_ready, r.value(2, 2))
                after(pe, kv_full, a.value(KC + 1, KC + 1) if a else (KC + 1) * B)
                parts = rows[:, par, :, 0:D].bitcast(F16)
                for c in range(KC):
                    for l in range(2):
                        for t in range(NT):
                            mm = pe.transpose(ps_x2t[:, c, l, t * P:(t + 1) * P],
                                              parts[:, t, l * D + c * P:l * D + (c + 1) * P], ident16[:])
                mm.then_inc(x2_turned, 1)

            def router(r, a):
                after(pe, x2t_ready, r.value(1, 1))
                after(pe, q_lo_ready, a.value(KC, KC) if a else KC * B)
                for t in range(NT):
                    mm = three(ps_logits[:, t, :],
                               lambda c: x2t[:, c, 0, t * P:(t + 1) * P], lambda c: x2t[:, c, 1, t * P:(t + 1) * P],
                               lambda c: r_hi[:, c, :], lambda c: r_lo[:, c, :], KC)
                mm.then_inc(logits_made, 1)

            def ranks(r):
                after(pe, both_ready, r.value(1, 1))
                pe.matmul(ps_ranks[0], before[:], both16[:, 0, :], start=True, stop=True)
                pe.matmul(ps_ranks[1], before[:], both16[:, 1, :], start=True, stop=False)
                pe.matmul(ps_ranks[1], ones16[:], both16[:, 0, :], start=False, stop=True)
                pe.matmul(ps_ranks[2], ones16[:], both16[:, 0, :], start=True, stop=False)
                pe.matmul(ps_ranks[2], ones16[:], both16[:, 1, :], start=False, stop=True).then_inc(ranks_made, 1)

            pe.wait_ge(const_ready, 10)
            pe.wait_ge(w_lo_ready, 5)

            def body(n, a, b, c, r):
                extra = {0: [(a, turn_x), (a, project_kv)],
                         1: [(c, turn_att), (a, project_q)],
                         2: [(r, lambda r: turn_x2(r, r.plus % 2, a))],
                         3: [(c, project_o), (r, lambda r: router(r, a))],
                         6: [(r, ranks)]}
                for u in range(UNITS):
                    if at := ahead(b, a, u + 2):
                        score(at[0], at[0].plus % 2, at[1])
                    if b:
                        turn_probs(b, u)
                    for at, stage in extra.get(u, []):
                        if at:
                            stage(at)
                    if b and u in LOW_ON_ACT:
                        take_high(b, u)
                    if b and u:
                        weigh_values(b, b.plus % 2, u - 1)
                if b:
                    weigh_values(b, b.plus % 2, UNITS - 1)

            batches(pe, body)

            def turn_rows(g):
                pe.wait_ge(raw_in, g * 16 + 16)
                parts = raw[:, :, 0:D].bitcast(F16)
                for c in range(KC):
                    for s in range(2):
                        for l in range(2):
                            mm = pe.transpose(ps_xt[c][:, l, s * P:(s + 1) * P],
                                              parts[:, s, l * D + c * P:l * D + (c + 1) * P], ident16[:])
                mm.then_inc(xg_turned, 1)

            def gate_up(g, parity, s):
                if s == 0:
                    pe.wait_ge(xg_act, g + 1)
                    pe.wait_ge(xg_vec, g + 1)
                if s >= 2:
                    pe.wait_ge(h_ready, g * STEPS + (s - 1))
                for k in range(2):
                    f = 2 * s + k
                    for m, dst in ((0, ps_gate[s % 2]), (1, ps_up[s % 2])):
                        at = lambda c: m * KC * F + c * F + f * P
                        mm = three(dst[:, k * TS:(k + 1) * TS],
                                   lambda c: e_hi[:, parity, at(c):at(c) + P], lambda c: e_lo[:, parity, at(c):at(c) + P],
                                   lambda c: xg[:, c, 0, :], lambda c: xg[:, c, 1, :], KC)
                mm.then_inc(gu_made, 1)

            def down(g, parity, s):
                pe.wait_ge(h_lo_ready, g * STEPS + (s + 1))
                if s == 0:
                    pe.wait_ge(y_ready, g * 2 + 1)
                for k in range(2):
                    f = 2 * s + k
                    at = 2 * KC * F + f * D
                    for half in range(2):
                        lhs = [h[:, f, half * P:(half + 1) * P] for h in (h_hi, h_lo)]
                        rhs = [w[:, parity, at:at + D] for w in (e_hi, e_lo)]
                        pe.matmul(ps_y[half][:, 0:D], lhs[0], rhs[0], start=f == 0, stop=False)
                        pe.matmul(ps_y[half][:, 0:D], lhs[0], rhs[1], start=False, stop=False)
                        mm = pe.matmul(ps_y[half][:, 0:D], lhs[1], rhs[0], start=False, stop=f == FC - 1)
                if s == STEPS - 1:
                    mm.then_inc(y_made, 1)

            turn_rows(0)
            pe.wait_ge(e_lo_ready, PIECES)
            gate_up(0, 0, 0)

            def tile(g, parity, parity_after):
                gate_up(g, parity, 1)
                down(g, parity, 0)
                gate_up(g, parity, 2)
                down(g, parity, 1)
                turn_rows(g + 1)
                gate_up(g, parity, 3)
                down(g, parity, 2)
                gate_up(g + 1, parity_after, 0)
                down(g, parity, 3)

            def tiles(e, parity, first, n):
                rest = pe.value_load(rest_i[0:1, bass.ds(e, 1)], min_val=1, max_val=T // TS - 1)
                last = pe.value_load(last_i[0:1, bass.ds(e, 1)], min_val=1, max_val=2 * T // TS + 2 * E)
                with pe.Fori(0, rest) as j:
                    tile(pe.snap(first + j), parity, parity)
                pe.wait_ge(e_lo_ready, e * PIECES + 2 * PIECES)
                tile(last, parity, 1 - parity)

            experts(pe, tiles)

        @block.scalar
        def _(act):
            for n in range(4):
                act.wait_ge(w_in, 64)
                act.activation(w_hi[:, n, :, :], w_stage[:, n, :, :], ACT.Copy, scale=WS).then_inc(w_hi_ready, 1)
            act.wait_ge(r_in, 80)
            act.activation(r_hi[:], r_stage[:], ACT.Copy, scale=WS).then_inc(w_hi_ready, 1)
            act.wait_ge(bias_ready, 3)

            def split_x(j):
                after(act, xt_turned, j.value(1, 1))
                after(act, q_made, j.value(1))
                act.activation(xt_hi[:].rearrange("p c s -> p (c s)"), ps_a[:], ACT.Copy).then_inc(xt_hi_ready, 1)

            def split_q(j, par):
                after(act, q_made, j.value(1, 1))
                after(act, s_made, j.value(UNITS, -UNITS))
                for m in range(KC):
                    act.activation(q_hi[:, par, m, :], ps_a[:, m * S:(m + 1) * S], ACT.Identity,
                                   bias=bq32[:, m:m + 1]).then_inc(q_hi_ready, 1)

            def exponentials(i, u):
                after(act, shifted, i.value(UNITS, u + 1))
                act.activation(probs[:, u % 2, :, :], probs[:, u % 2, :, :], ACT.Exp, scale=S_SCALE).then_inc(exp_ready, 1)

            def split_probs(i, u):
                after(act, p_turned, i.value(UNITS, u + 1))
                after(act, pv_made, i.value(UNITS, u - 1))
                act.activation(pt_hi[:, u % 2, :], ps_probs[u % 2][0:KS, :], ACT.Copy).then_inc(pt_hi_ready, 1)

            def split_att(j):
                after(act, at_turned, j.value(1, 1))
                after(act, o_made, j.value(1))
                act.activation(at_hi[:].rearrange("p c s -> p (c s)"), ps_c[:], ACT.Copy).then_inc(at_hi_ready, 1)

            def copy_x2(r):
                after(act, x2_turned, r.value(1, 1))
                act.activation(x2t[:].rearrange("p c l s -> p (c l s)"), ps_x2t[:].rearrange("p c l s -> p (c l s)"),
                               ACT.Copy).then_inc(x2t_ready, 1)

            def router_exp(r):
                after(act, shift_ready, r.value(1, 1))
                act.activation(expl[:], expl[:], ACT.Exp, scale=1.0 / WS).then_inc(expl_ready, 1)

            def low_probs(i, u):
                after(act, p_rest, i.value(len(LOW_ON_ACT), of_act(u)))
                act.activation(pt_lo[:, u % 2, :], ps_probs[u % 2][0:KS, :], ACT.Copy).then_inc(lo_by_act, 1)

            def norm(j, which, src, dst, turned, per, ready, m):
                after(act, ln, m.value(LN_STEPS, LN_STEPS))
                after(act, turned, j.value(per))
                for t in range(NT):
                    at = which * NT + t
                    act.activation(dst[:, t, :], src[:, t, :], ACT.Identity, bias=ln_bias[:, at:at + 1],
                                   scale=ln_rstd[:, at:at + 1]).then_inc(ready, 1)

            def body(n, a, b, c, r):
                m = n or (c and c + 3)
                extra = {0: [(a, split_x)],
                         1: [(c, split_att), (a, lambda j: split_q(j, j.plus % 2))],
                         2: [(r, copy_x2)], 5: [(r, router_exp)],
                         7: [(n, lambda j: norm(j, 0, xin, xn, xt_turned, 1, xn_ready, m)),
                             (c, lambda j: norm(j, 1, x2, x2n, row_ready, 2, x2n_ready, m))]}
                for u in range(UNITS):
                    if b:
                        split_probs(b, u)
                    if at := ahead(b, a, u + 1):
                        exponentials(*at)
                    for at, stage in extra.get(u, []):
                        if at:
                            stage(at)
                    if b and u in LOW_ON_ACT:
                        low_probs(b, u)

            batches(act, body)

            def split_weights(e, parity, n):
                cols = slice(n * PIECE, (n + 1) * PIECE)
                act.activation(e_hi[:, parity, cols], e_stage[:, cols], ACT.Copy, scale=WS).then_inc(e_hi_ready, 1)

            act.wait_ge(e_in, 48)
            for n in range(PIECES):
                split_weights(0, 0, n)
            act.wait_ge(e_lo_ready, PIECES)
            load_expert(act, 1)
            act.wait_ge(xg_turned, 1)
            act.activation(xg[:, 0, :, :], ps_xt[0], ACT.Copy).then_inc(xg_act, 1)

            def silu_step(g, s):
                act.wait_ge(gu_made, g * STEPS + (s + 1))
                if s == STEPS - 1:
                    act.wait_ge(xg_turned, g + 2)
                    act.activation(xg[:, 0, :, :], ps_xt[0], ACT.Copy).then_inc(xg_act, 1)
                act.activation(g_act[:, s % 2, :], ps_gate[s % 2][:], ACT.Silu, scale=1.0 / WS).then_inc(silu_ready, 1)
                act.wait_ge(h_ready, g * STEPS + (s + 1))
                act.activation(h_hi[:, 2 * s:2 * s + 2, :].rearrange("p f t -> p (f t)"), h_full[:, s % 2, :],
                               ACT.Copy).then_inc(h_hi_ready, 1)

            def tile(g, e, parity, prepare):
                for n, s in enumerate((1, 2, 3, 0)):
                    silu_step(g if s else g + 1, s)
                    if prepare:
                        if n == 0:
                            act.wait_ge(e_in, e * 48 + 96)
                        for piece in range(3 * n, 3 * n + 3):
                            split_weights(e + 1, 1 - parity, piece)

            silu_step(0, 0)

            def tiles(e, parity, first, n):
                tile(first, e, parity, True)
                act.wait_ge(e_lo_ready, e * PIECES + 2 * PIECES)
                load_expert(act, (e + 2) % E)
                with act.Fori(1, n) as j:
                    tile(act.snap(first + j), e, parity, False)

            experts(act, tiles)
            act.wait_ge(e_in, 48 * (E + 2))

        @block.vector
        def _(dve):
            def twos(ap):
                return ap.unsqueeze(2)

            for n in range(4):
                dve.wait_ge(w_hi_ready, n + 1)
                dve.scalar_tensor_tensor(w_lo[:, n, :, :].rearrange("p c e -> p (c e)"),
                                         w_stage[:, n, :, :].rearrange("p c e -> p (c e)"), WS,
                                         w_hi[:, n, :, :].rearrange("p c e -> p (c e)"), ALU.mult, ALU.subtract).then_inc(w_lo_ready, 1)
            dve.wait_ge(w_hi_ready, 5)
            dve.scalar_tensor_tensor(r_lo[:], r_stage[:], WS, r_hi[:], ALU.mult, ALU.subtract).then_inc(w_lo_ready, 1)
            dve.wait_ge(r_in, 80)
            for full, scaled in ((bq, bq32), (bk, bk32), (bv, bv32)):
                dve.tensor_scalar(scaled[:], full[:], WS, None, ALU.mult).then_inc(bias_ready, 1)
            dve.memset(ln_mv[:], 0.0).then_inc(bias_ready, 1)
            dve.wait_ge(const_ready, 10)
            dve.tensor_copy(expert_f[:], expert_i[:]).then_inc(bias_ready, 1)
            dve.tensor_copy(next_row[:], region_i[:]).then_inc(bias_ready, 1)
            dve.wait_ge(bias_ready, 6)

            def statistics(m, n, c):
                parts = [(0, t, xin) for t in range(NT)] * bool(n) + [(1, t, x2) for t in range(NT)] * bool(c)
                cols = slice(0 if n else NT, 2 * NT if c else NT)
                var, tmp, rstd, bias, mv = ln_var[:, cols], ln_tmp[:, cols], ln_rstd[:, cols], ln_bias[:, cols], ln_mv[:, cols, :]
                done = 0

                def step(ins):
                    nonlocal done
                    ins.then_inc(ln, 1)
                    done += 1

                def settle():
                    after(dve, ln, m.value(LN_STEPS, done))

                if n:
                    after(dve, x_in, n.value(16, 16))
                if c:
                    after(dve, x2_ready, c.value(1, 1))
                for which, t, src in parts:
                    ins = dve.bn_stats(ln_stats[:, which * NT + t, :], src[:, t, :])
                step(ins)
                yield
                settle()
                apart(dve, passed)
                for which, t, _ in parts:
                    ins = dve.bn_aggr(ln_mv[:, which * NT + t, :], ln_stats[:, which * NT + t, :])
                step(ins)
                yield
                settle()
                step(dve.tensor_scalar(var, mv[:, :, 1], EPS, None, ALU.add))
                yield
                settle()
                step(dve.tensor_scalar(tmp.bitcast(I32), var.bitcast(I32), 1, None, ALU.logical_shift_right))
                yield
                settle()
                if n:
                    after(dve, xn_ready, n.value(NT))
                if c:
                    after(dve, x2n_ready, c.value(NT))
                step(dve.tensor_scalar(rstd.bitcast(I32), tmp.bitcast(I32), -1.0, float(RSQRT_SEED), ALU.mult, ALU.add))
                for _ in range(3):
                    yield
                    settle()
                    step(dve.tensor_tensor(tmp, rstd, rstd, ALU.mult))
                    yield
                    settle()
                    step(dve.scalar_tensor_tensor(tmp, tmp, -0.5, var, ALU.mult, ALU.mult))
                    yield
                    settle()
                    step(dve.scalar_tensor_tensor(rstd, tmp, 1.5, rstd, ALU.add, ALU.mult))
                yield
                settle()
                step(dve.scalar_tensor_tensor(bias, mv[:, :, 0], -1.0, rstd, ALU.mult, ALU.mult))
                assert done == LN_STEPS

            def low_x(j):
                after(dve, xt_hi_ready, j.value(1, 1))
                dve.tensor_tensor(xt_lo[:].rearrange("p c s -> p (c s)"), ps_a[:], xt_hi[:].rearrange("p c s -> p (c s)"),
                                  ALU.subtract).then_inc(xt_lo_ready, 1)

            def full_kv(j):
                after(dve, kv_made, j.value(1, 1))
                after(dve, kv_part, j.value(4))
                for m in range(KC):
                    dve.tensor_scalar(k_full[:, m, :], ps_kv[:, m * KS:(m + 1) * KS], bk32[:, m:m + 1], None,
                                      ALU.add).then_inc(kv_full, 1)
                dve.tensor_tensor(v_full[:], ps_kv[0:KS, KC * KS:KC * KS + D], bv32[:], ALU.add).then_inc(kv_full, 1)

            def low_q(j, par):
                after(dve, q_hi_ready, j.value(KC, KC))
                for m in range(KC):
                    dve.scalar_tensor_tensor(q_lo[:, par, m, :], ps_a[:, m * S:(m + 1) * S], bq32[:, m:m + 1],
                                             q_hi[:, par, m, :], ALU.add, ALU.subtract).then_inc(q_lo_ready, 1)

            def shift(i, u, between):
                after(dve, s_made, i.value(UNITS, u + 1))
                scores = ps_score[u % 2][:, 0:HG * KS].rearrange("p (h k) -> p h k", h=HG)
                dve.tensor_reduce(row_max[:, u % 2, :], scores, AX.X, ALU.max).then_inc(max_ready, 1)
                between()
                after(dve, max_ready, i.value(UNITS, u + 1))
                after(dve, p_turned, i.value(UNITS, u - 1))
                dve.tensor_tensor(probs[:, u % 2, :, :], scores, twos(row_max[:, u % 2, :]).broadcast_to([P, HG, KS]),
                                  ALU.subtract).then_inc(shifted, 1)
                between()

            def low_probs(i, u):
                after(dve, pt_hi_ready, i.value(UNITS, u + 1))
                dve.tensor_tensor(pt_lo[:, u % 2, :], ps_probs[u % 2][0:KS, :], pt_hi[:, u % 2, :],
                                  ALU.subtract).then_inc(lo_by_dve, 1)

            def normalize(i, t):
                heads = ps_att[:, 0:H * VW].rearrange("p (h w) -> p h w", h=H)
                after(dve, pv_made, i.value(UNITS, (t + 1) * UNITS // NT))
                dve.reciprocal(inv_sum[:], heads[:, :, DK]).then_inc(inv_ready, 1)
                after(dve, inv_ready, i.value(NT, t + 1))
                after(dve, at_turned, i.value(1))
                dve.tensor_tensor(att[:, t, :].rearrange("p (h w) -> p h w", h=H), heads[:, :, 0:DK],
                                  twos(inv_sum[:]).broadcast_to([P, H, DK]), ALU.mult).then_inc(att_ready, 1)

            def low_att(j):
                after(dve, at_hi_ready, j.value(1, 1))
                dve.tensor_tensor(at_lo[:].rearrange("p c s -> p (c s)"), ps_c[:], at_hi[:].rearrange("p c s -> p (c s)"),
                                  ALU.subtract).then_inc(at_lo_ready, 1)

            def residual(j):
                after(dve, o_made, j.value(1, 1))
                after(dve, xb_ready, j.value(1, 1))
                after(dve, x2_out, j.value(16))
                dve.scalar_tensor_tensor(x2[:].rearrange("p t d -> p (t d)"), ps_c[:], 1.0 / (WS * WS),
                                         xres[:].rearrange("p t d -> p (t d)"), ALU.mult, ALU.add).then_inc(x2_ready, 1)

            dve.sem_inc(slots_ready, 1)

            def wide(ap):
                return ap.unsqueeze(2).broadcast_to([P, NT, E])

            def route_top(r):
                done = 0

                def step(ins):
                    nonlocal done
                    ins.then_inc(route, 1)
                    done += 1

                def settle():
                    after(dve, route, r.value(ROUTE, done))

                after(dve, logits_made, r.value(1, 1))
                apart(dve, passed)
                for t in range(NT):
                    ins = dve.max(top[:, t, :], ps_logits[:, t, :])
                step(ins)
                yield
                settle()
                dve.tensor_tensor(expl[:], ps_logits, wide(top[:, :, 0]), ALU.subtract).then_inc(shift_ready, 1)
                apart(dve, passed)
                for t in range(NT):
                    ins = dve.max_index(top_at[:, t, :], top[:, t, :], ps_logits[:, t, :])
                step(ins)
                yield
                settle()
                step(dve.tensor_tensor(pick[:], expert_f[:].unsqueeze(1).unsqueeze(2).broadcast_to([P, NT, 2, E]),
                                       top_at[:, :, 0:2].unsqueeze(3).broadcast_to([P, NT, 2, E]), ALU.is_equal))
                yield
                settle()
                dve.tensor_tensor(both16[:], pick[:, :, 0, :], pick[:, :, 1, :], ALU.add).then_inc(both_ready, 1)

            def combine_weights(r, par):
                after(dve, expl_ready, r.value(1, 1))
                done = 0

                def step(ins):
                    nonlocal done
                    ins.then_inc(route_w, 1)
                    done += 1

                step(dve.tensor_reduce(prob_sum[:], expl[:], AX.X, ALU.add))
                yield
                after(dve, route_w, r.value(3, done))
                step(dve.reciprocal(prob_inv[:], prob_sum[:]))
                yield
                after(dve, route_w, r.value(3, done))
                after(dve, both_ready, r.value(1, 1))
                step(dve.tensor_tensor(weight[:], both16[:], wide(prob_inv[:]), ALU.mult))
                yield
                after(dve, route_w, r.value(3, done))
                after(dve, row_ready, r.value(2, 2))
                dve.tensor_tensor(rows[:, par, :, D:D + E], weight[:], expl[:], ALU.mult).then_inc(cw_ready, 1)

            def take_slots(r, par):
                after(dve, ranks_made, r.value(1, 1))
                done = 0

                def step(ins):
                    nonlocal done
                    ins.then_inc(route_s, 1)
                    done += 1

                def settle():
                    after(dve, route_s, r.value(4, done))

                step(dve.tensor_tensor(slot[:], ps_rank_pair, next_row[:].unsqueeze(1).broadcast_to([P, NT, E]), ALU.add))
                yield
                settle()
                step(dve.tensor_tensor(next_row[:], ps_ranks[NT], next_row[:], ALU.add))
                yield
                settle()
                step(dve.tensor_tensor(slot_of[:], pick[:], slot[:].unsqueeze(2).broadcast_to([P, NT, 2, E]), ALU.mult))
                yield
                settle()
                step(dve.tensor_reduce(slot_f[:], slot_of[:], AX.X, ALU.add))
                yield
                settle()
                dve.tensor_copy(slot_u[:, par, :, :], slot_f[:]).then_inc(slots_ready, 1)

            def body(n, a, b, c, r):
                m = n or (c and c + 3)
                under_way = []

                def between():
                    for chain in under_way:
                        next(chain, None)

                def finish(chain):
                    for _ in chain:
                        pass

                def start(chain):
                    under_way.append(chain)

                top_chain = route_top(r) if r else iter(())
                extra = {0: [(c, lambda j: normalize(j, 1)), (a, low_x)],
                         1: [(a, full_kv)],
                         2: [(a, lambda j: low_q(j, j.plus % 2)), (c, low_att)],
                         3: [(c, residual), (m, lambda j: start(statistics(j, n, c)))],
                         4: [(r, lambda j: start(top_chain)), (b, lambda j: normalize(j, 0))],
                         6: [(r, lambda j: finish(top_chain)), (r, lambda j: start(combine_weights(j, j.plus % 2)))],
                         7: [(r, lambda j: start(take_slots(j, j.plus % 2)))]}
                for u in range(UNITS):
                    if at := ahead(b, a, u + 1):
                        shift(*at, between)
                    for at, stage in extra.get(u, []):
                        if at:
                            stage(at)
                            between()
                    if b and u not in LOW_ON_ACT:
                        low_probs(b, u)
                        between()
                while under_way:
                    under_way = [chain for chain in under_way if next(chain, False) is None]

            batches(dve, body)

            dve.wait_ge(slots_ready, B + 1)
            done = 0

            def step(ins):
                nonlocal done
                ins.then_inc(counted, 1)
                done += 1
                dve.wait_ge(counted, done)

            step(dve.tensor_copy(count_f[:], region_i[0:1, :]))
            step(dve.tensor_tensor(count_f[:], next_row[0:1, :], count_f[:], ALU.subtract))
            step(dve.tensor_scalar(tiles_f[:], count_f[:], float(TS - 1), 1.0 / TS, ALU.add, ALU.mult))
            step(dve.tensor_scalar(tiles_f[:], tiles_f[:], (TS - 1) / (2.0 * TS), 2.0, ALU.subtract, ALU.max))
            dve.tensor_copy(tiles_i[:], tiles_f[:]).then_inc(tables_ready, 1)
            dve.tensor_copy(pad_i[:], next_row[0:1, :]).then_inc(tables_ready, 1)
            dve.wait_ge(tables_ready, 2)
            step(dve.tensor_copy(tiles_g[:], tiles_i[:]))
            step(dve.memset(base_a[:], 0.0))
            step(dve.tensor_copy(base_a[:, 1:E], tiles_g[:, 0:E - 1]))
            src, dst = base_a, base_b
            for by in (1, 2, 4):
                step(dve.tensor_copy(dst[:, 0:by], src[:, 0:by]))
                step(dve.tensor_tensor(dst[:, by:E], src[:, by:E], src[:, 0:E - by], ALU.add))
                src, dst = dst, src
            dve.tensor_copy(base_i[:], src[:]).then_inc(tables_ready, 1)
            step(dve.tensor_scalar(rest_f[:], tiles_g[:], -1.0, None, ALU.add))
            dve.tensor_copy(rest_i[:], rest_f[:]).then_inc(tables_ready, 1)
            dve.tensor_tensor(last_i[:], src[:], rest_f[:], ALU.add).then_inc(tables_ready, 1)
            dve.wait_ge(tables_ready, 5)

            def low_weights(e, parity, n):
                cols = slice(n * PIECE, (n + 1) * PIECE)
                dve.wait_ge(e_hi_ready, e * PIECES + (n + 1))
                dve.scalar_tensor_tensor(e_lo[:, parity, cols], e_stage[:, cols], WS, e_hi[:, parity, cols],
                                         ALU.mult, ALU.subtract).then_inc(e_lo_ready, 1)

            dve.memset(w_row[:], 0.0).then_inc(raw_free, 1)
            dve.memset(y_sb[:], 0.0).then_inc(y_ready, 1)
            for n in range(PIECES):
                low_weights(0, 0, n)

            def h_step(g, s):
                if s == STEPS - 1:
                    dve.wait_ge(gu_made, g * STEPS + STEPS)
                    dve.wait_ge(xg_turned, g + 2)
                    dve.tensor_copy(xg[:, 1, :, :], ps_xt[1]).then_inc(xg_vec, 1)
                    take_rows(g + 1)
                dve.wait_ge(silu_ready, g * STEPS + (s + 1))
                dve.scalar_tensor_tensor(h_full[:, s % 2, :], ps_up[s % 2][:], H_DOWN, g_act[:, s % 2, :],
                                         ALU.mult, ALU.mult).then_inc(h_ready, 1)
                dve.wait_ge(h_hi_ready, g * STEPS + (s + 1))
                dve.tensor_tensor(h_lo[:, 2 * s:2 * s + 2, :].rearrange("p f t -> p (f t)"), h_full[:, s % 2, :],
                                  h_hi[:, 2 * s:2 * s + 2, :].rearrange("p f t -> p (f t)"), ALU.subtract).then_inc(h_lo_ready, 1)

            def take_rows(g):
                dve.tensor_copy(tail_in[:], raw[:, :, D:RW]).then_inc(raw_free, 1)

            dve.wait_ge(xg_turned, 1)
            dve.tensor_copy(xg[:, 1, :, :], ps_xt[1]).then_inc(xg_vec, 1)
            take_rows(0)
            h_step(0, 0)

            def tile(g, e, parity, prepare):
                for n, s in enumerate((1, 2, 3, 0)):
                    if s == STEPS - 1:
                        dve.wait_ge(added, g * 32 + 16)
                        dve.wait_ge(raw_free, g + 2)
                        dve.tensor_copy(tok_row[:], tail_in[:, :, E].bitcast(U32)).then_inc(meta_ready, 1)
                        dve.tensor_copy(w_row[:], tail_in[:, :, bass.ds(e, 1)].rearrange("p s w -> p (s w)")).then_inc(meta_ready, 1)
                        dve.wait_ge(meta_ready, g * 2 + 2)
                    h_step(g if s else g + 1, s)
                    if prepare:
                        for piece in range(3 * n, 3 * n + 3):
                            low_weights(e + 1, 1 - parity, piece)
                dve.wait_ge(y_made, g + 1)
                for half in range(2):
                    dve.tensor_scalar(y_sb[:, half, :], ps_y[half][:, 0:D], w_row[:, half:half + 1], 8.0 / WS,
                                      ALU.mult, ALU.mult).then_inc(y_ready, 1)

            def tiles(e, parity, first, n):
                tile(first, e, parity, True)
                with dve.Fori(1, n) as j:
                    tile(dve.snap(first + j), e, parity, False)

            experts(dve, tiles)

        @block.gpsimd
        def _(pool):
            pool.memset(ident[:], 0.0).then_inc(const_base, 1)
            pool.memset(ident16[:], 0.0).then_inc(const_base, 1)
            pool.memset(minus16[:], 0.0).then_inc(const_base, 1)
            pool.memset(before[:], 1.0).then_inc(const_base, 1)
            pool.memset(head_mask[:], 1.0).then_inc(const_base, 1)
            pool.memset(pads[:], 0.0).then_inc(const_base, 1)
            pool.wait_ge(const_base, 6)
            pool.affine_select(out=ident[:], in_=ident[:], compare_op=ALU.not_equal, fill=1.0, base=0,
                               pattern=[[-1, P]], channel_multiplier=1).then_inc(const_ready, 1)
            pool.affine_select(out=ident16[:], in_=ident16[:], compare_op=ALU.not_equal, fill=1.0, base=0,
                               pattern=[[-1, P]], channel_multiplier=1).then_inc(const_ready, 1)
            pool.affine_select(out=minus16[:], in_=minus16[:], compare_op=ALU.not_equal, fill=-1.0, base=0,
                               pattern=[[-1, P]], channel_multiplier=1).then_inc(const_ready, 1)
            pool.affine_select(out=before[:], in_=before[:], compare_op=ALU.is_ge, fill=0.0, base=-1,
                               pattern=[[1, P]], channel_multiplier=-1).then_inc(const_ready, 1)
            pool.affine_select(out=head_mask[:], in_=head_mask[:], compare_op=ALU.is_ge, fill=0.0, base=0,
                               pattern=[[-DK, P // DK]], channel_multiplier=1).then_inc(const_base, 1)
            pool.wait_ge(const_base, 7)
            pool.affine_select(out=head_mask[:], in_=head_mask[:], compare_op=ALU.is_ge, fill=0.0, base=DK - 1,
                               pattern=[[DK, P // DK]], channel_multiplier=-1).then_inc(const_ready, 1)
            pool.memset(ones16[:], 1.0).then_inc(const_ready, 1)
            pool.iota(expert_i[:], pattern=[[1, E]], base=0, channel_multiplier=0).then_inc(const_ready, 1)
            pool.iota(region_i[:], pattern=[[REGION, E]], base=0, channel_multiplier=0).then_inc(const_ready, 1)
            pool.iota(token_i[:], pattern=[[P, NT]], base=0, channel_multiplier=1).then_inc(const_ready, 1)
            pool.iota(pads[:, :, RW - 1].bitcast(I32), pattern=[[P, 2]], base=T, channel_multiplier=1).then_inc(const_ready, 1)
            for par in range(2):
                pool.memset(v_parts[:, par, 0, :, DK:VW], 1.0).then_inc(ones_set, 1)
                pool.memset(v_parts[:, par, 1, :, DK:VW], 0.0).then_inc(ones_set, 1)
            pool.wait_ge(const_ready, 10)
            pool.wait_ge(ones_set, 4)
            pool.dma_start(out[T:T + P, :], pads[:, 0, 0:D]).then_inc(added, 16)
            pool.dma_start(out[T + P:T + TS, :], pads[:, 1, 0:D]).then_inc(scattered, 16)

            def split_cx(j):
                after(pool, cx_in, j.value(16, 16))
                after(pool, kv_made, j.value(1))
                apart(pool, passed)
                pool.tensor_copy(cx_hi[:], cx[:]).then_inc(cx_hi_ready, 1)
                after(pool, cx_hi_ready, j.value(1, 1))
                pool.tensor_tensor(cx_lo[:], cx[:], cx_hi[:], ALU.subtract).then_inc(cx_lo_ready, 1)

            def split_kv(j, par):
                after(pool, kv_full, j.value(KC + 1, KC + 1))
                after(pool, kd_ready, j.value(1))
                apart(pool, passed)
                pool.tensor_copy(k_parts[:, 0, :, :], k_full[:]).then_inc(kv_part, 1)
                after(pool, pv_made, j.value(UNITS, -UNITS))
                v_heads = v_full[:].rearrange("k (h w) -> k h w", h=H)
                apart(pool, passed)
                pool.tensor_copy(v_parts[:, par, 0, :, 0:DK], v_heads).then_inc(kv_part, 1)
                after(pool, kv_part, j.value(4, 2))
                pool.tensor_tensor(k_parts[:, 1, :, :], k_full[:], k_parts[:, 0, :, :], ALU.subtract).then_inc(kv_part, 1)
                pool.tensor_tensor(v_parts[:, par, 1, :, 0:DK], v_heads, v_parts[:, par, 0, :, 0:DK], ALU.subtract).then_inc(kv_part, 1)
                after(pool, kv_part, j.value(4, 4))
                heads = P // DK
                pool.tensor_tensor(k_diag[:, par].rearrange("p l c h k -> p (l c) h k"),
                                   k_parts[:].rearrange("p l c k -> p (l c) k").unsqueeze(2).broadcast_to([P, 2 * KC, heads, KS]),
                                   head_mask[:].unsqueeze(1).unsqueeze(3).broadcast_to([P, 2 * KC, heads, KS]),
                                   ALU.mult).then_inc(kd_ready, 1)

            def add_bias(j):
                after(pool, xres_in, j.value(16, 16))
                pool.tensor_tensor(xres[:], xres[:], bo[:].unsqueeze(1).broadcast_to([P, NT, D]), ALU.add).then_inc(xb_ready, 1)

            def make_rows(j, par):
                after(pool, x2n_ready, j.value(NT, NT))
                after(pool, scattered, j.value(SCATTER, 16 - SCATTER))
                parts = rows[:, par, :, 0:D].bitcast(F16)
                apart(pool, passed)
                pool.tensor_copy(parts[:, :, 0:D], x2n[:]).then_inc(row_hi_ready, 1)
                pool.tensor_copy(rows[:, par, :, RW - 1].bitcast(I32), token_i[:]).then_inc(row_ready, 1)
                after(pool, row_hi_ready, j.value(1, 1))
                after(pool, row_ready, j.value(2, 1))
                pool.tensor_tensor(parts[:, :, D:2 * D], x2n[:], parts[:, :, 0:D], ALU.subtract).then_inc(row_ready, 1)
                pool.tensor_scalar(token_i[:], token_i[:], float(S), None, ALU.add).then_inc(token_ready, 1)
                after(pool, token_ready, j.value(1, 1))

            def scatter(r, par):
                after(pool, row_ready, r.value(2, 2))
                after(pool, cw_ready, r.value(1, 1))
                after(pool, slots_ready, r.value(1, 2))
                apart(pool, passed)
                for t in range(NT):
                    for k in range(2):
                        pool.indirect_dma_start(rows_dram, bass.IndirectOffsetOnAxis(slot_u[:, par, t, k:k + 1], 0),
                                                rows[:, par, t, :], None).then_inc(scattered, 16)

            def body(n, a, b, c, r):
                if a:
                    split_kv(a, a.plus % 2)
                if n:
                    split_cx(n)
                if b:
                    add_bias(b)
                if c:
                    make_rows(c, c.plus % 2)
                if r:
                    scatter(r, r.plus % 2)

            pool.wait_ge(r_in, 80)
            batches(pool, body)

            pool.wait_ge(x2_out, 16 * B)
            pool.wait_ge(tables_ready, 5)

            def tiles(e, parity, first, n):
                with pool.Fori(0, n) as j:
                    g = pool.snap(first + j)
                    pool.wait_ge(added, g * 32 + 16)
                    pool.wait_ge(meta_ready, g * 2 + 2)
                    for half in range(2):
                        pool.wait_ge(y_ready, g * 2 + (half + 2))
                        apart(pool, passed)
                        pool.indirect_dma_start(out, bass.IndirectOffsetOnAxis(tok_row[:, half:half + 1], 0),
                                                y_sb[:, half, :], None, compute_op=ALU.add).then_inc(added, 16)

            experts(pool, tiles)


def kernel(**inputs):
    import concourse.bacc as bacc
    from concourse.bass_utils import run_bass_kernel_spmd

    g = {n: np.asarray(a) for n, a in inputs.items()}
    turned = lambda a: np.ascontiguousarray(np.swapaxes(a, -1, -2))
    columns = lambda a: a.reshape(KC, P).T
    arrays = {
        "x": np.ascontiguousarray(g["x"].reshape(T, D)),
        "ctx_t": turned(g["ctx_1024"]),
        "w_q": turned(g["L0_xattn_w_q"]), "b_q": columns(g["L0_xattn_b_q"]),
        "w_k": turned(g["L0_xattn_w_k"]), "b_k": columns(g["L0_xattn_b_k"]),
        "w_v": turned(g["L0_xattn_w_v"]), "b_v": g["L0_xattn_b_v"],
        "w_o": turned(g["L0_xattn_w_o"]), "b_o": g["L0_xattn_b_o"],
        "router_w": g["L0_ffn_router_w"], "gate_w": g["L0_ffn_gate_w"],
        "up_w": g["L0_ffn_up_w"], "down_w": g["L0_ffn_down_w"],
    }
    nc = bacc.Bacc("TRN2", target_bir_lowering=False, num_devices=1)
    arrays = {f"in_{n}": np.ascontiguousarray(a) for n, a in arrays.items()}
    args = [nc.dram_tensor(n, a.shape, mybir.dt.from_np(a.dtype), kind="ExternalInput").ap() for n, a in arrays.items()]
    args.append(nc.dram_tensor("out_0", (T + TS, D), F32, kind="ExternalOutput").ap())
    build(nc, *args)
    result = run_bass_kernel_spmd(nc, [arrays], core_ids=[0])
    return result.results[0]["out_0"][0:T].reshape(B, S, D)
```

```python
from contextlib import ExitStack

import numpy as np
import concourse.bass as bass
from concourse import mybir
from concourse.alu_op_type import AluOpType as ALU

F32 = mybir.dt.float32
F16 = mybir.dt.float16
I32 = mybir.dt.int32
U32 = mybir.dt.uint32
ACT = mybir.ActivationFunctionType
AX = mybir.AxisListType

P = 128
B, S, D = 16, 256, 256
KS = 77
H, DK = 16, 16
E, F = 8, 1024
T = B * S
KC = D // P
NT = S // P
FC = F // P
HG = 4
UNITS = NT * H // HG
VW = DK + 1
EPS = 1e-5
WS = 32.0
S_SCALE = 1.0 / (WS * WS * 4.0)
H_DOWN = 1.0 / 256.0
TS = 256
PAD = 2 * TS
REGION = T + PAD
RW = D + E + 1
WCOLS = 3 * KC * F
PIECE = 512
PIECES = WCOLS // PIECE
EARLY = 8
PIECES_AT = (0, 3, 7, 9, 12)
STEPS = FC // 2
RSQRT_SEED = 0x5F3759DF
LN_STEPS = 1 + 3 + 9 + 1
LOW_ON_ACT = (0, 1, 2, 3, 4, 5, 6)
ROUTE = 3
STAGES = 6
SCATTER = 2 * NT * 16


class At:

    def __init__(self, plus, reg=None, times=0):
        self.plus, self.reg, self.times = plus, reg, times

    def __add__(self, n):
        return At(self.plus + n, self.reg, self.times)

    def __sub__(self, n):
        return self + (-n)

    def value(self, per, k=0):
        n = per * self.plus + k
        return n if self.reg is None else self.reg * (per * self.times) + n


def after(eng, sem, value):
    if not isinstance(value, int) or value > 0:
        eng.wait_ge(sem, value)


def apart(eng, passed):
    eng.sem_inc(passed, 1)


def build(nc, x, ctx_t, w_q, b_q, w_k, b_k, w_v, b_v, w_o, b_o, router_w, gate_w, up_w, down_w, out):
    rows_dram = nc.dram_tensor("expert_rows", (E * REGION, RW), F32, kind="Internal").ap()
    x_tiles = x.rearrange("(b t p) d -> b p t d", t=NT, p=P)
    out_tiles = out[0:T, :].rearrange("(b t p) d -> b p t d", t=NT, p=P)

    with ExitStack() as stack:
        def sb(name, shape, dt=F32):
            return stack.enter_context(nc.sbuf_tensor(name, shape, dt))

        def bank(name):
            return stack.enter_context(nc.psum_tensor(name, [P, 512], F32))

        def sem(name):
            return stack.enter_context(nc.semaphore(name))

        ident = sb("ident", [P, P])
        ident16 = sb("ident16", [P, P], F16)
        before = sb("before", [P, P], F16)
        ones16 = sb("ones16", [P, P], F16)
        minus16 = sb("minus16", [P, P], F16)
        head_mask = sb("head_mask", [P, P // DK], F16)
        expert_i = sb("expert_i", [P, E], I32)
        expert_f = sb("expert_f", [P, E])
        region_i = sb("region_i", [P, E], I32)
        token_i = sb("token_i", [P, NT], I32)
        pads = sb("pads", [P, 2, RW])
        w_stage = sb("w_stage", [P, 4, KC, D])
        w_hi = sb("w_hi", [P, 4, KC, D], F16)
        w_lo = sb("w_lo", [P, 4, KC, D], F16)
        r_stage = sb("r_stage", [P, KC, E])
        r_hi = sb("r_hi", [P, KC, E], F16)
        r_lo = sb("r_lo", [P, KC, E], F16)
        bq = sb("bq", [P, KC])
        bk = sb("bk", [P, KC])
        bq32 = sb("bq32", [P, KC])
        bk32 = sb("bk32", [P, KC])
        bv = sb("bv", [KS, D])
        bv32 = sb("bv32", [KS, D])
        bo = sb("bo", [P, D])
        xin = sb("xin", [P, NT, D])
        xn = sb("xn", [P, NT, D])
        ln_stats = sb("ln_stats", [P, 2 * NT, 6])
        ln_mv = sb("ln_mv", [P, 2 * NT, 2])
        ln_var = sb("ln_var", [P, 2 * NT])
        ln_tmp = sb("ln_tmp", [P, 2 * NT])
        ln_rstd = sb("ln_rstd", [P, 2 * NT])
        ln_bias = sb("ln_bias", [P, 2 * NT])
        xt_hi = sb("xt_hi", [P, KC, S], F16)
        xt_lo = sb("xt_lo", [P, KC, S], F16)
        q_hi = sb("q_hi", [P, 2, KC, S], F16)
        q_lo = sb("q_lo", [P, 2, KC, S], F16)
        cx = sb("cx", [P, KC, KS])
        cx_hi = sb("cx_hi", [P, KC, KS], F16)
        cx_lo = sb("cx_lo", [P, KC, KS], F16)
        k_full = sb("k_full", [P, KC, KS])
        v_full = sb("v_full", [KS, D])
        k_parts = sb("k_parts", [P, 2, KC, KS], F16)
        k_diag = sb("k_diag", [P, 2, 2, KC, P // DK, KS], F16)
        v_parts = sb("v_parts", [KS, 2, 2, H, VW], F16)
        row_max = sb("row_max", [P, 2, HG])
        probs = sb("probs", [P, 2, HG, KS])
        pt_hi = sb("pt_hi", [KS, 2, HG * P], F16)
        pt_lo = sb("pt_lo", [KS, 2, HG * P], F16)
        inv_sum = sb("inv_sum", [P, H])
        att = sb("att", [P, NT, D])
        at_hi = sb("at_hi", [P, KC, S], F16)
        at_lo = sb("at_lo", [P, KC, S], F16)
        xres = sb("xres", [P, NT, D])
        x2 = sb("x2", [P, NT, D])
        x2n = sb("x2n", [P, NT, D])
        x2t = sb("x2t", [P, KC, 2, S], F16)
        rows = sb("rows", [P, 2, NT, RW])
        expl = sb("expl", [P, NT, E])
        top = sb("top", [P, NT, E])
        top_at = sb("top_at", [P, NT, E], U32)
        pick = sb("pick", [P, NT, 2, E])
        both16 = sb("both16", [P, NT, E], F16)
        prob_sum = sb("prob_sum", [P, NT])
        prob_inv = sb("prob_inv", [P, NT])
        weight = sb("weight", [P, NT, E])
        next_row = sb("next_row", [P, E])
        slot = sb("slot", [P, NT, E])
        slot_of = sb("slot_of", [P, NT, 2, E])
        slot_f = sb("slot_f", [P, NT, 2])
        slot_u = sb("slot_u", [P, 2, NT, 2], U32)
        count_f = sb("count_f", [1, E])
        tiles_f = sb("tiles_f", [1, E])
        tiles_i = sb("tiles_i", [1, E], I32)
        tiles_g = sb("tiles_g", [1, E])
        base_a = sb("base_a", [1, E])
        base_b = sb("base_b", [1, E])
        base_i = sb("base_i", [1, E], I32)
        pad_i = sb("pad_i", [1, E], I32)
        rest_f = sb("rest_f", [1, E])
        rest_i = sb("rest_i", [1, E], I32)
        spare_f = sb("spare_f", [1, E])
        half_f = sb("half_f", [1, E])
        half_i = sb("half_i", [1, E], I32)
        e_stage = sb("e_stage", [P, WCOLS])
        e_hi = sb("e_hi", [P, 2, WCOLS], F16)
        e_lo = sb("e_lo", [P, 2, WCOLS], F16)
        raw = sb("raw", [P, 2, RW])
        tail_in = sb("tail_in", [P, 2, E + 1])
        xg = sb("xg", [P, KC, 2, TS], F16)
        g_act = sb("g_act", [P, 2, 512])
        h_full = sb("h_full", [P, 2, 512])
        h_hi = sb("h_hi", [P, FC, TS], F16)
        h_lo = sb("h_lo", [P, FC, TS], F16)
        w_row = sb("w_row", [P, 2])
        tok_row = sb("tok_row", [P, 2], U32)
        y_sb = sb("y_sb", [P, 2, D])

        banks = [bank(f"bank{n}") for n in range(8)]
        ps_score = [banks[0], banks[1]]
        ps_probs = [banks[2], banks[3]]
        ps_att, ps_a, ps_r, ps_c = banks[4:8]
        ps_logits = ps_r[:, 0:NT * E].rearrange("p (t e) -> p t e", t=NT)
        ps_ranks = [ps_r[:, (NT + n) * E:(NT + n + 1) * E] for n in range(NT + 1)]
        ps_rank_pair = ps_r[:, NT * E:2 * NT * E].rearrange("p (t e) -> p t e", t=NT)
        ps_x2t = ps_r[:].bitcast(F16).rearrange("p (c l s) -> p c l s", c=KC, l=2)
        ps_gate = [banks[0], banks[1]]
        ps_up = [banks[2], banks[3]]
        ps_y = [banks[4], banks[5]]
        ps_xt = [banks[6 + c][:, 0:TS].bitcast(F16).rearrange("p (l s) -> p l s", l=2) for c in range(KC)]

        passed = sem("passed")
        w_in = sem("w_in")
        r_in = sem("r_in")
        e_in = sem("e_in")
        w_hi_ready = sem("w_hi_ready")
        w_lo_ready = sem("w_lo_ready")
        bias_ready = sem("bias_ready")
        const_base = sem("const_base")
        const_ready = sem("const_ready")
        x_in = sem("x_in")
        xres_in = sem("xres_in")
        cx_in = sem("cx_in")
        xn_ready = sem("xn_ready")
        xt_turned = sem("xt_turned")
        xt_hi_ready = sem("xt_hi_ready")
        xt_lo_ready = sem("xt_lo_ready")
        q_made = sem("q_made")
        q_hi_ready = sem("q_hi_ready")
        q_lo_ready = sem("q_lo_ready")
        cx_hi_ready = sem("cx_hi_ready")
        cx_lo_ready = sem("cx_lo_ready")
        kv_made = sem("kv_made")
        kv_full = sem("kv_full")
        k_part = sem("k_part")
        v_part = sem("v_part")
        kd_ready = sem("kd_ready")
        s_made = sem("s_made")
        max_ready = sem("max_ready")
        shifted = sem("shifted")
        exp_ready = sem("exp_ready")
        p_turned = sem("p_turned")
        pt_hi_ready = sem("pt_hi_ready")
        p_rest = sem("p_rest")
        lo_by_act = sem("lo_by_act")
        lo_by_dve = sem("lo_by_dve")
        pv_made = sem("pv_made")
        inv_ready = sem("inv_ready")
        att_ready = sem("att_ready")
        at_turned = sem("at_turned")
        at_hi_ready = sem("at_hi_ready")
        at_lo_ready = sem("at_lo_ready")
        o_made = sem("o_made")
        xb_ready = sem("xb_ready")
        x2_ready = sem("x2_ready")
        x_summed = sem("x_summed")
        x2_summed = sem("x2_summed")
        ln = sem("ln")
        x2n_ready = sem("x2n_ready")
        x2_turned = sem("x2_turned")
        x2t_ready = sem("x2t_ready")
        logits_made = sem("logits_made")
        route = sem("route")
        route_w = sem("route_w")
        route_s = sem("route_s")
        ones_set = sem("ones_set")
        token_ready = sem("token_ready")
        shift_ready = sem("shift_ready")
        expl_ready = sem("expl_ready")
        both_ready = sem("both_ready")
        ranks_made = sem("ranks_made")
        cw_ready = sem("cw_ready")
        slots_ready = sem("slots_ready")
        row_hi_ready = sem("row_hi_ready")
        row_ready = sem("row_ready")
        scattered = sem("scattered")
        x2_out = sem("x2_out")
        counted = sem("counted")
        tables_ready = sem("tables_ready")
        pad_out = sem("pad_out")
        raw_in = sem("raw_in")
        raw_free = sem("raw_free")
        xg_turned = sem("xg_turned")
        xg_act = sem("xg_act")
        xg_vec = sem("xg_vec")
        gu_made = sem("gu_made")
        silu_ready = sem("silu_ready")
        h_ready = sem("h_ready")
        h_hi_ready = sem("h_hi_ready")
        h_lo_ready = sem("h_lo_ready")
        y_made = sem("y_made")
        meta_ready = sem("meta_ready")
        y_ready = sem("y_ready")
        added = sem("added")
        e_hi_ready = sem("e_hi_ready")
        e_lo_ready = sem("e_lo_ready")

        block = stack.enter_context(nc.Block())

        def load_expert(eng, e):
            for m, w in enumerate((gate_w, up_w)):
                eng.dma_start(e_stage[:, m * KC * F:(m + 1) * KC * F].rearrange("p (c f) -> p c f", c=KC),
                              w[bass.ds(e, 1), :, :].rearrange("a (c p) f -> p (a c) f", p=P)).then_inc(e_in, 16)
            eng.dma_start(e_stage[:, 2 * KC * F:].rearrange("p (c d) -> p c d", c=FC),
                          down_w[bass.ds(e, 1), :, :].rearrange("a (c p) d -> p (a c) d", p=P)).then_inc(e_in, 16)

        def batches(eng, body):
            for first in range(STAGES):
                body(*[At(first - stage) if first >= stage else None for stage in range(STAGES)])
            with eng.Fori(0, (B - STAGES) // 2) as k:
                for odd in range(2):
                    body(*[At(STAGES + odd - stage, k, 2) for stage in range(STAGES)])
            for first in range(B, B + STAGES - 1):
                body(*[At(first - stage) if first - stage < B else None for stage in range(STAGES)])

        def early_pieces(c, r):
            return range(EARLY) if r and not c else ()

        def unit(c, b, a, u):
            at, v = (c, u + UNITS) if u < 0 else (b, u) if u < UNITS else (a, u - UNITS)
            return (at, v) if at else None

        def low_done(eng, i, u):
            back, v = divmod(u, UNITS)
            on_act = v in LOW_ON_ACT
            done = [w for w in range(v + 1) if (w in LOW_ON_ACT) == on_act]
            per = len(LOW_ON_ACT) if on_act else UNITS - len(LOW_ON_ACT)
            after(eng, lo_by_act if on_act else lo_by_dve, i.value(per, per * back + len(done)))

        def of_act(u):
            return len([w for w in LOW_ON_ACT if w <= u])

        def experts(eng, body, counts=None):
            counts = tiles_i if counts is None else counts
            with eng.Fori(0, E // 2) as pair:
                for parity in range(2):
                    e = pair * 2 + parity
                    n = eng.value_load(counts[0:1, bass.ds(e, 1)], min_val=1, max_val=T // TS)
                    first = eng.value_load(base_i[0:1, bass.ds(e, 1)], min_val=0, max_val=2 * T // TS + 2 * E)
                    body(e, parity, first, n)

        @block.sync
        def _(sp):
            for n, w in enumerate((w_q, w_k, w_v, w_o)):
                sp.dma_start(w_stage[:, n, :, :], w.rearrange("(c p) e -> p c e", p=P)).then_inc(w_in, 16)
            sp.dma_start(xin[:], x_tiles[0]).then_inc(x_in, 16)
            sp.dma_start(cx[:], ctx_t[0].rearrange("(c p) k -> p c k", p=P)).then_inc(cx_in, 16)
            sp.dma_start(bq[:], b_q).then_inc(r_in, 16)
            sp.dma_start(bk[:], b_k).then_inc(r_in, 16)
            sp.dma_start(bv[:], b_v.partition_broadcast(KS)).then_inc(r_in, 16)
            sp.dma_start(bo[:], b_o.partition_broadcast(P)).then_inc(r_in, 16)
            sp.dma_start(r_stage[:], router_w.rearrange("(c p) e -> p c e", p=P)).then_inc(r_in, 16)
            sp.dma_start(xres[:], x_tiles[0]).then_inc(xres_in, 16)
            load_expert(sp, 0)

            def load_a(j):
                after(sp, xn_ready, j.value(NT))
                sp.dma_start(xin[:], x_tiles[bass.ds(j.value(1), 1)].rearrange("a p t d -> p (a t) d")).then_inc(x_in, 16)
                after(sp, cx_lo_ready, j.value(1))
                sp.dma_start(cx[:], ctx_t[bass.ds(j.value(1), 1)].rearrange("a (c p) k -> p (a c) k", p=P)).then_inc(cx_in, 16)

            def store_c(j):
                after(sp, x2_ready, j.value(1, 1))
                sp.dma_start(out_tiles[bass.ds(j.value(1), 1)].rearrange("a p t d -> p (a t) d"), x2[:]).then_inc(x2_out, 16)

            def load_c(j):
                after(sp, x2_ready, j.value(1))
                sp.dma_start(xres[:], x_tiles[bass.ds(j.value(1), 1)].rearrange("a p t d -> p (a t) d")).then_inc(xres_in, 16)

            load_a(At(1))
            load_a(At(2))
            with sp.Fori(0, B - 3) as k:
                load_a(At(3, k, 1))
                store_c(At(0, k, 1))
                load_c(At(1, k, 1))
            for j in range(B - 3, B):
                store_c(At(j))
                if j + 1 < B:
                    load_c(At(j + 1))

            def pad_expert(e):
                at = sp.value_load(pad_i[0:1, bass.ds(e, 1)], min_val=0, max_val=E * REGION - PAD)
                for half in range(PAD // TS):
                    sp.dma_start(rows_dram[bass.ds(at + half * TS, TS), :].rearrange("(s p) w -> p s w", p=P),
                                 pads[:]).then_inc(pad_out, 16)

            sp.wait_ge(tables_ready, 5)
            sp.wait_ge(const_ready, 10)
            pad_expert(0)
            sp.wait_ge(scattered, SCATTER * B)
            sp.wait_ge(pad_out, 16 * PAD // TS)
            sp.dma_start(raw[:], rows_dram[0:TS, :].rearrange("(s p) w -> p s w", p=P)).then_inc(raw_in, 16)
            sp.wait_ge(e_lo_ready, PIECES)
            load_expert(sp, 1)

            def load_rows(e, free, j):
                sp.wait_ge(raw_free, free)
                sp.dma_start(raw[:], rows_dram[bass.ds(e * REGION + j * TS, TS), :].rearrange(
                    "(s p) w -> p s w", p=P)).then_inc(raw_in, 16)

            def tiles(e, parity, first, rest):
                pad_expert((e + 1) % E)
                with sp.Fori(0, rest) as j:
                    load_rows(e, first + j + 2, j + 1)
                sp.wait_ge(e_lo_ready, e * PIECES + 2 * PIECES)
                apart(sp, passed)
                load_expert(sp, (e + 2) % E)
                sp.wait_ge(pad_out, e * (16 * PAD // TS) + 2 * (16 * PAD // TS))
                apart(sp, passed)
                load_rows((e + 1) % E, first + rest + 2, 0)

            experts(sp, tiles, rest_i)
            total = sp.value_load(base_i[0:1, E - 1:E], min_val=0, max_val=2 * T // TS + 2 * E)
            last = sp.value_load(tiles_i[0:1, E - 1:E], min_val=2, max_val=T // TS)
            sp.wait_ge(pad_out, (E + 1) * 16 * PAD // TS)
            sp.wait_ge(raw_in, (total + last) * 16 + 16)
            sp.wait_ge(x2_out, 16 * B)
            sp.wait_ge(added, (total + last) * 32 + 16)
            apart(sp, passed)

        @block.tensor
        def _(pe):
            def three(dst, a_hi, a_lo, b_hi, b_lo, chunks):
                for c in range(chunks):
                    pe.matmul(dst, a_hi(c), b_hi(c), start=c == 0, stop=False)
                    pe.matmul(dst, a_hi(c), b_lo(c), start=False, stop=False)
                    mm = pe.matmul(dst, a_lo(c), b_hi(c), start=False, stop=c == chunks - 1)
                return mm

            def turn_x(j):
                after(pe, xn_ready, j.value(NT, NT))
                after(pe, kv_full, j.value(KC + 1, KC + 1))
                for t in range(NT):
                    for c in range(KC):
                        mm = pe.transpose(ps_a[:, c * S + t * P:c * S + (t + 1) * P], xn[:, t, c * P:(c + 1) * P], ident[:])
                mm.then_inc(xt_turned, 1)

            def project_kv(j):
                after(pe, cx_lo_ready, j.value(1, 1))
                after(pe, q_lo_ready, j.value(KC))
                for m in range(KC):
                    three(ps_a[:, m * KS:(m + 1) * KS],
                          lambda c: w_hi[:, 1, c, m * P:(m + 1) * P], lambda c: w_lo[:, 1, c, m * P:(m + 1) * P],
                          lambda c: cx_hi[:, c, :], lambda c: cx_lo[:, c, :], KC)
                three(ps_a[0:KS, KC * KS:KC * KS + D], lambda c: cx_hi[:, c, :], lambda c: cx_lo[:, c, :],
                      lambda c: w_hi[:, 2, c, :], lambda c: w_lo[:, 2, c, :], KC).then_inc(kv_made, 1)

            def project_q(j):
                after(pe, xt_lo_ready, j.value(1, 1))
                for m in range(KC):
                    mm = three(ps_a[:, m * S:(m + 1) * S],
                               lambda c: w_hi[:, 0, c, m * P:(m + 1) * P], lambda c: w_lo[:, 0, c, m * P:(m + 1) * P],
                               lambda c: xt_hi[:, c, :], lambda c: xt_lo[:, c, :], KC)
                mm.then_inc(q_made, 1)

            def score(i, par, u):
                t, v = divmod(u, UNITS // NT)
                m, half = divmod(v, 2)
                if u == 0:
                    after(pe, q_lo_ready, i.value(KC, KC))
                    after(pe, kd_ready, i.value(1, 1))
                after(pe, shifted, i.value(UNITS, u - 1))
                keys = [k_diag[:, par, l, m, half * HG:(half + 1) * HG, :].rearrange("p h k -> p (h k)") for l in range(2)]
                three(ps_score[u % 2][:, 0:HG * KS],
                      lambda c: q_hi[:, par, m, t * P:(t + 1) * P], lambda c: q_lo[:, par, m, t * P:(t + 1) * P],
                      lambda c: keys[0], lambda c: keys[1], 1).then_inc(s_made, 1)

            def turn_probs(i, u):
                after(pe, exp_ready, i.value(UNITS, u + 1))
                low_done(pe, i, u - 2)
                for h in range(HG):
                    mm = pe.matmul(ps_probs[u % 2][0:KS, h * P:(h + 1) * P], probs[:, u % 2, h, :], ident[:], is_transpose=True,
                                   start=h == 0, stop=h == HG - 1)
                mm.then_inc(p_turned, 1)

            def take_high(i, u):
                after(pe, pt_hi_ready, i.value(UNITS, u + 1))
                pe.matmul(ps_probs[u % 2][0:KS, :], minus16[0:KS, 0:KS], pt_hi[:, u % 2, :],
                          start=False, stop=True, skip_group_check=True).then_inc(p_rest, 1)

            def weigh_values(i, par, u):
                t, v = divmod(u, UNITS // NT)
                if u == 0:
                    after(pe, v_part, i.value(2, 2))
                if v == 0:
                    after(pe, att_ready, i.value(NT, t))
                low_done(pe, i, u)
                for g in range(HG):
                    h = v * HG + g
                    mm = three(ps_att[:, h * VW:(h + 1) * VW],
                               lambda c: pt_hi[:, u % 2, g * P:(g + 1) * P], lambda c: pt_lo[:, u % 2, g * P:(g + 1) * P],
                               lambda c: v_parts[:, par, 0, h, :], lambda c: v_parts[:, par, 1, h, :], 1)
                mm.then_inc(pv_made, 1)

            def turn_att(j):
                after(pe, att_ready, j.value(NT, NT))
                after(pe, x2_ready, j.value(1))
                for t in range(NT):
                    for c in range(KC):
                        mm = pe.transpose(ps_c[:, c * S + t * P:c * S + (t + 1) * P], att[:, t, c * P:(c + 1) * P], ident[:])
                mm.then_inc(at_turned, 1)

            def project_o(j):
                after(pe, at_lo_ready, j.value(1, 1))
                for t in range(NT):
                    mm = three(ps_c[:, t * D:(t + 1) * D],
                               lambda c: at_hi[:, c, t * P:(t + 1) * P], lambda c: at_lo[:, c, t * P:(t + 1) * P],
                               lambda c: w_hi[:, 3, c, :], lambda c: w_lo[:, 3, c, :], KC)
                mm.then_inc(o_made, 1)

            def turn_x2(r, par):
                after(pe, row_ready, r.value(2, 2))
                after(pe, slots_ready, r.value(1))
                parts = rows[:, par, :, 0:D].bitcast(F16)
                for c in range(KC):
                    for l in range(2):
                        for t in range(NT):
                            mm = pe.transpose(ps_x2t[:, c, l, t * P:(t + 1) * P],
                                              parts[:, t, l * D + c * P:l * D + (c + 1) * P], ident16[:])
                mm.then_inc(x2_turned, 1)

            def router(r):
                after(pe, x2t_ready, r.value(1, 1))
                for t in range(NT):
                    mm = three(ps_logits[:, t, :],
                               lambda c: x2t[:, c, 0, t * P:(t + 1) * P], lambda c: x2t[:, c, 1, t * P:(t + 1) * P],
                               lambda c: r_hi[:, c, :], lambda c: r_lo[:, c, :], KC)
                mm.then_inc(logits_made, 1)

            def ranks(r):
                after(pe, both_ready, r.value(1, 1))
                pe.matmul(ps_ranks[0], before[:], both16[:, 0, :], start=True, stop=True)
                pe.matmul(ps_ranks[1], before[:], both16[:, 1, :], start=True, stop=False)
                pe.matmul(ps_ranks[1], ones16[:], both16[:, 0, :], start=False, stop=True)
                pe.matmul(ps_ranks[2], ones16[:], both16[:, 0, :], start=True, stop=False)
                pe.matmul(ps_ranks[2], ones16[:], both16[:, 1, :], start=False, stop=True).then_inc(ranks_made, 1)

            pe.wait_ge(const_ready, 10)
            pe.wait_ge(w_lo_ready, 5)

            def body(n, a, b, c, r, z):
                extra = {0: [(z, ranks)],
                         1: [(a, turn_x), (c, turn_att)],
                         2: [(a, project_q)],
                         3: [(c, project_o)],
                         4: [(r, lambda r: turn_x2(r, r.plus % 2))],
                         5: [(r, router)],
                         7: [(n, project_kv)]}
                for u in range(UNITS):
                    if at := unit(c, b, a, u + 2):
                        score(at[0], at[0].plus % 2, at[1])
                    if (at := unit(c, b, a, u - 1)) and at[1] in LOW_ON_ACT:
                        take_high(*at)
                    if at := unit(c, b, a, u - 2):
                        weigh_values(at[0], at[0].plus % 2, at[1])
                    if b:
                        turn_probs(b, u)
                    for at, stage in extra.get(u, []):
                        if at:
                            stage(at)

            batches(pe, body)

            def turn_rows(g):
                pe.wait_ge(raw_in, g * 16 + 16)
                parts = raw[:, :, 0:D].bitcast(F16)
                for c in range(KC):
                    for s in range(2):
                        for l in range(2):
                            mm = pe.transpose(ps_xt[c][:, l, s * P:(s + 1) * P],
                                              parts[:, s, l * D + c * P:l * D + (c + 1) * P], ident16[:])
                mm.then_inc(xg_turned, 1)

            def gate_up(g, parity, s, rows=TS):
                if s == 0:
                    pe.wait_ge(xg_act, g + 1)
                    pe.wait_ge(xg_vec, g + 1)
                if s >= 2:
                    pe.wait_ge(h_ready, g * STEPS + (s - 1))
                for k in range(2):
                    f = 2 * s + k
                    for m, dst in ((0, ps_gate[s % 2]), (1, ps_up[s % 2])):
                        at = lambda c: m * KC * F + c * F + f * P
                        mm = three(dst[:, k * TS:k * TS + rows],
                                   lambda c: e_hi[:, parity, at(c):at(c) + P], lambda c: e_lo[:, parity, at(c):at(c) + P],
                                   lambda c: xg[:, c, 0, 0:rows], lambda c: xg[:, c, 1, 0:rows], KC)
                mm.then_inc(gu_made, 1)

            def down(g, parity, s, rows=TS):
                pe.wait_ge(h_lo_ready, g * STEPS + (s + 1))
                if s == 0:
                    pe.wait_ge(y_ready, g * 2 + 1)
                for k in range(2):
                    f = 2 * s + k
                    at = 2 * KC * F + f * D
                    for half in range(rows // P):
                        lhs = [h[:, f, half * P:(half + 1) * P] for h in (h_hi, h_lo)]
                        rhs = [w[:, parity, at:at + D] for w in (e_hi, e_lo)]
                        pe.matmul(ps_y[half][:, 0:D], lhs[0], rhs[0], start=f == 0, stop=False)
                        pe.matmul(ps_y[half][:, 0:D], lhs[0], rhs[1], start=False, stop=False)
                        mm = pe.matmul(ps_y[half][:, 0:D], lhs[1], rhs[0], start=False, stop=f == FC - 1)
                if s == STEPS - 1:
                    mm.then_inc(y_made, 1)

            turn_rows(0)
            pe.wait_ge(e_lo_ready, PIECES)
            gate_up(0, 0, 0)

            def tile(g, parity, parity_after, rows=TS):
                gate_up(g, parity, 1, rows)
                down(g, parity, 0, rows)
                gate_up(g, parity, 2, rows)
                down(g, parity, 1, rows)
                turn_rows(g + 1)
                gate_up(g, parity, 3, rows)
                down(g, parity, 2, rows)
                gate_up(g + 1, parity_after, 0)
                down(g, parity, 3, rows)

            def tiles(e, parity, first, rest):
                half = pe.value_load(half_i[0:1, bass.ds(e, 1)], min_val=0, max_val=1)
                with pe.Fori(0, rest) as j:
                    tile(pe.snap(first + j), parity, parity)
                pe.wait_ge(e_lo_ready, e * PIECES + 2 * PIECES)
                last = pe.snap(first + rest)
                with pe.If(half == 1):
                    tile(last, parity, 1 - parity, P)
                with pe.Else():
                    tile(last, parity, 1 - parity)

            experts(pe, tiles, rest_i)

        @block.scalar
        def _(act):
            for n in range(4):
                act.wait_ge(w_in, 64)
                act.activation(w_hi[:, n, :, :], w_stage[:, n, :, :], ACT.Copy, scale=WS).then_inc(w_hi_ready, 1)
            act.wait_ge(r_in, 80)
            act.activation(r_hi[:], r_stage[:], ACT.Copy, scale=WS).then_inc(w_hi_ready, 1)
            act.wait_ge(bias_ready, 3)

            def split_x(j):
                after(act, xt_turned, j.value(1, 1))
                after(act, q_made, j.value(1))
                act.activation(xt_hi[:].rearrange("p c s -> p (c s)"), ps_a[:], ACT.Copy).then_inc(xt_hi_ready, 1)

            def split_q(j, par):
                after(act, q_made, j.value(1, 1))
                after(act, s_made, j.value(UNITS, -UNITS))
                for m in range(KC):
                    act.activation(q_hi[:, par, m, :], ps_a[:, m * S:(m + 1) * S], ACT.Identity,
                                   bias=bq32[:, m:m + 1]).then_inc(q_hi_ready, 1)

            def exponentials(i, u):
                after(act, shifted, i.value(UNITS, u + 1))
                act.activation(probs[:, u % 2, :, :], probs[:, u % 2, :, :], ACT.Exp, scale=S_SCALE).then_inc(exp_ready, 1)

            def split_probs(i, u):
                after(act, p_turned, i.value(UNITS, u + 1))
                after(act, pv_made, i.value(UNITS, u - 1))
                act.activation(pt_hi[:, u % 2, :], ps_probs[u % 2][0:KS, :], ACT.Copy).then_inc(pt_hi_ready, 1)

            def split_att(j):
                after(act, at_turned, j.value(1, 1))
                after(act, o_made, j.value(1))
                act.activation(at_hi[:].rearrange("p c s -> p (c s)"), ps_c[:], ACT.Copy).then_inc(at_hi_ready, 1)

            def copy_x2(r):
                after(act, x2_turned, r.value(1, 1))
                act.activation(x2t[:].rearrange("p c l s -> p (c l s)"), ps_x2t[:].rearrange("p c l s -> p (c l s)"),
                               ACT.Copy).then_inc(x2t_ready, 1)

            def split_weights(e, parity, n):
                cols = slice(n * PIECE, (n + 1) * PIECE)
                act.activation(e_hi[:, parity, cols], e_stage[:, cols], ACT.Copy, scale=WS).then_inc(e_hi_ready, 1)

            def split_early(pieces):
                act.wait_ge(e_in, 48)
                for n in pieces:
                    split_weights(0, 0, n)

            def router_exp(r):
                after(act, shift_ready, r.value(1, 1))
                act.activation(expl[:], expl[:], ACT.Exp, scale=1.0 / WS).then_inc(expl_ready, 1)

            def low_probs(i, u):
                after(act, p_rest, i.value(len(LOW_ON_ACT), of_act(u)))
                act.activation(pt_lo[:, u % 2, :], ps_probs[u % 2][0:KS, :], ACT.Copy).then_inc(lo_by_act, 1)

            def norm(j, which, src, dst, used, per, ready, m):
                after(act, ln, m.value(LN_STEPS, LN_STEPS))
                after(act, used, j.value(per))
                for t in range(NT):
                    at = which * NT + t
                    act.activation(dst[:, t, :], src[:, t, :], ACT.Identity, bias=ln_bias[:, at:at + 1],
                                   scale=ln_rstd[:, at:at + 1]).then_inc(ready, 1)

            def body(n, a, b, c, r, z):
                m = a or (r and r + 3)
                early = early_pieces(c, r)
                extra = {0: [(a, lambda j: norm(j, 0, xin, xn, xt_turned, 1, xn_ready, m))],
                         1: [(a, split_x), (c, split_att)],
                         2: [(r, lambda j: norm(j, 1, x2, x2n, row_ready, 2, x2n_ready, m))],
                         3: [(a, lambda j: split_q(j, j.plus % 2))],
                         4: [(early, split_early), (r, copy_x2)],
                         7: [(r, router_exp)]}
                for u in range(UNITS):
                    if (at := unit(c, b, a, u - 1)) and at[1] in LOW_ON_ACT:
                        low_probs(*at)
                    if at := unit(c, b, a, u + 1):
                        exponentials(*at)
                    if b:
                        split_probs(b, u)
                    for at, stage in extra.get(u, []):
                        if at:
                            stage(at)

            batches(act, body)

            split_early(range(EARLY, PIECES))
            act.wait_ge(xg_turned, 1)
            act.activation(xg[:, 0, :, :], ps_xt[0], ACT.Copy).then_inc(xg_act, 1)

            def silu_step(g, s):
                act.wait_ge(gu_made, g * STEPS + (s + 1))
                if s == STEPS - 1:
                    act.wait_ge(xg_turned, g + 2)
                    act.activation(xg[:, 0, :, :], ps_xt[0], ACT.Copy).then_inc(xg_act, 1)
                act.activation(g_act[:, s % 2, :], ps_gate[s % 2][:], ACT.Silu, scale=1.0 / WS).then_inc(silu_ready, 1)
                act.wait_ge(h_ready, g * STEPS + (s + 1))
                act.activation(h_hi[:, 2 * s:2 * s + 2, :].rearrange("p f t -> p (f t)"), h_full[:, s % 2, :],
                               ACT.Copy).then_inc(h_hi_ready, 1)

            def tile(g, e, parity, prepare):
                for n, s in enumerate((1, 2, 3, 0)):
                    silu_step(g if s else g + 1, s)
                    if prepare:
                        if n == 0:
                            act.wait_ge(e_in, e * 48 + 96)
                        for piece in range(PIECES_AT[n], PIECES_AT[n + 1]):
                            split_weights(e + 1, 1 - parity, piece)

            silu_step(0, 0)

            def tiles(e, parity, first, n):
                tile(first, e, parity, True)
                with act.Fori(1, n) as j:
                    tile(act.snap(first + j), e, parity, False)

            experts(act, tiles)
            act.wait_ge(e_in, 48 * (E + 2))

        @block.vector
        def _(dve):
            def twos(ap):
                return ap.unsqueeze(2)

            for n in range(4):
                dve.wait_ge(w_hi_ready, n + 1)
                dve.scalar_tensor_tensor(w_lo[:, n, :, :].rearrange("p c e -> p (c e)"),
                                         w_stage[:, n, :, :].rearrange("p c e -> p (c e)"), WS,
                                         w_hi[:, n, :, :].rearrange("p c e -> p (c e)"), ALU.mult, ALU.subtract).then_inc(w_lo_ready, 1)
            dve.wait_ge(w_hi_ready, 5)
            dve.scalar_tensor_tensor(r_lo[:], r_stage[:], WS, r_hi[:], ALU.mult, ALU.subtract).then_inc(w_lo_ready, 1)
            dve.wait_ge(r_in, 80)
            for full, scaled in ((bq, bq32), (bk, bk32), (bv, bv32)):
                dve.tensor_scalar(scaled[:], full[:], WS, None, ALU.mult).then_inc(bias_ready, 1)
            dve.memset(ln_mv[:], 0.0).then_inc(bias_ready, 1)
            dve.wait_ge(const_ready, 10)
            dve.tensor_copy(expert_f[:], expert_i[:]).then_inc(bias_ready, 1)
            dve.tensor_copy(next_row[:], region_i[:]).then_inc(bias_ready, 1)
            dve.wait_ge(bias_ready, 6)

            def sum_x(j, which, src, come, per, ready):
                after(dve, come, j.value(per, per))
                for t in range(NT):
                    ins = dve.bn_stats(ln_stats[:, which * NT + t, :], src[:, t, :])
                ins.then_inc(ready, 1)

            def statistics(m, n, c):
                cols = slice(0 if n else NT, 2 * NT if c else NT)
                var, tmp, rstd, bias, mv = ln_var[:, cols], ln_tmp[:, cols], ln_rstd[:, cols], ln_bias[:, cols], ln_mv[:, cols, :]
                done = 0

                def step(ins):
                    nonlocal done
                    ins.then_inc(ln, 1)
                    done += 1

                def settle():
                    after(dve, ln, m.value(LN_STEPS, done))

                if n:
                    after(dve, x_summed, n.value(1, 1))
                if c:
                    after(dve, x2_summed, c.value(1, 1))
                apart(dve, passed)
                for at in range(2 * NT)[cols]:
                    ins = dve.bn_aggr(ln_mv[:, at, :], ln_stats[:, at, :])
                step(ins)
                yield
                settle()
                step(dve.tensor_scalar(var, mv[:, :, 1], EPS, None, ALU.add))
                yield
                settle()
                step(dve.tensor_scalar(tmp.bitcast(I32), var.bitcast(I32), 1, None, ALU.logical_shift_right))
                yield
                settle()
                if n:
                    after(dve, xn_ready, n.value(NT))
                if c:
                    after(dve, x2n_ready, c.value(NT))
                step(dve.tensor_scalar(rstd.bitcast(I32), tmp.bitcast(I32), -1.0, float(RSQRT_SEED), ALU.mult, ALU.add))
                for _ in range(3):
                    yield
                    settle()
                    step(dve.tensor_tensor(tmp, rstd, rstd, ALU.mult))
                    yield
                    settle()
                    step(dve.scalar_tensor_tensor(tmp, tmp, -0.5, var, ALU.mult, ALU.mult))
                    yield
                    settle()
                    step(dve.scalar_tensor_tensor(rstd, tmp, 1.5, rstd, ALU.add, ALU.mult))
                yield
                settle()
                step(dve.scalar_tensor_tensor(bias, mv[:, :, 0], -1.0, rstd, ALU.mult, ALU.mult))
                assert done == LN_STEPS

            def low_x(j):
                after(dve, xt_hi_ready, j.value(1, 1))
                dve.tensor_tensor(xt_lo[:].rearrange("p c s -> p (c s)"), ps_a[:], xt_hi[:].rearrange("p c s -> p (c s)"),
                                  ALU.subtract).then_inc(xt_lo_ready, 1)

            def full_kv(j):
                after(dve, kv_made, j.value(1, 1))
                after(dve, k_part, j.value(2))
                after(dve, v_part, j.value(2))
                for m in range(KC):
                    dve.tensor_scalar(k_full[:, m, :], ps_a[:, m * KS:(m + 1) * KS], bk32[:, m:m + 1], None,
                                      ALU.add).then_inc(kv_full, 1)
                dve.tensor_tensor(v_full[:], ps_a[0:KS, KC * KS:KC * KS + D], bv32[:], ALU.add).then_inc(kv_full, 1)

            def high_rows(r, par):
                after(dve, x2n_ready, r.value(NT, NT))
                after(dve, scattered, r.value(SCATTER, -SCATTER))
                dve.tensor_copy(rows[:, par, :, 0:D].bitcast(F16)[:, :, 0:D], x2n[:]).then_inc(row_hi_ready, 1)

            def low_q(j, par):
                after(dve, q_hi_ready, j.value(KC, KC))
                for m in range(KC):
                    dve.scalar_tensor_tensor(q_lo[:, par, m, :], ps_a[:, m * S:(m + 1) * S], bq32[:, m:m + 1],
                                             q_hi[:, par, m, :], ALU.add, ALU.subtract).then_inc(q_lo_ready, 1)

            def scores(u):
                return ps_score[u % 2][:, 0:HG * KS].rearrange("p (h k) -> p h k", h=HG)

            def maximum(i, u):
                after(dve, s_made, i.value(UNITS, u + 1))
                dve.tensor_reduce(row_max[:, u % 2, :], scores(u), AX.X, ALU.max).then_inc(max_ready, 1)

            def shift(i, u):
                after(dve, max_ready, i.value(UNITS, u + 1))
                after(dve, p_turned, i.value(UNITS, u - 1))
                dve.tensor_tensor(probs[:, u % 2, :, :], scores(u), twos(row_max[:, u % 2, :]).broadcast_to([P, HG, KS]),
                                  ALU.subtract).then_inc(shifted, 1)

            def low_probs(i, u):
                after(dve, pt_hi_ready, i.value(UNITS, u + 1))
                dve.tensor_tensor(pt_lo[:, u % 2, :], ps_probs[u % 2][0:KS, :], pt_hi[:, u % 2, :],
                                  ALU.subtract).then_inc(lo_by_dve, 1)

            def normalize(i, t):
                heads = ps_att[:, 0:H * VW].rearrange("p (h w) -> p h w", h=H)
                after(dve, pv_made, i.value(UNITS, (t + 1) * UNITS // NT))
                dve.reciprocal(inv_sum[:], heads[:, :, DK]).then_inc(inv_ready, 1)
                after(dve, inv_ready, i.value(NT, t + 1))
                after(dve, at_turned, i.value(1))
                dve.tensor_tensor(att[:, t, :].rearrange("p (h w) -> p h w", h=H), heads[:, :, 0:DK],
                                  twos(inv_sum[:]).broadcast_to([P, H, DK]), ALU.mult).then_inc(att_ready, 1)

            def low_att(j):
                after(dve, at_hi_ready, j.value(1, 1))
                dve.tensor_tensor(at_lo[:].rearrange("p c s -> p (c s)"), ps_c[:], at_hi[:].rearrange("p c s -> p (c s)"),
                                  ALU.subtract).then_inc(at_lo_ready, 1)

            def residual(j):
                after(dve, o_made, j.value(1, 1))
                after(dve, xb_ready, j.value(1, 1))
                after(dve, x2_out, j.value(16))
                after(dve, x2n_ready, j.value(NT))
                dve.scalar_tensor_tensor(x2[:].rearrange("p t d -> p (t d)"), ps_c[:], 1.0 / (WS * WS),
                                         xres[:].rearrange("p t d -> p (t d)"), ALU.mult, ALU.add).then_inc(x2_ready, 1)

            def wide(ap):
                return ap.unsqueeze(2).broadcast_to([P, NT, E])

            def route_top(r):
                done = 0

                def step(ins):
                    nonlocal done
                    ins.then_inc(route, 1)
                    done += 1

                def settle():
                    after(dve, route, r.value(ROUTE, done))

                after(dve, logits_made, r.value(1, 1))
                apart(dve, passed)
                for t in range(NT):
                    ins = dve.max(top[:, t, :], ps_logits[:, t, :])
                step(ins)
                yield
                settle()
                dve.tensor_tensor(expl[:], ps_logits, wide(top[:, :, 0]), ALU.subtract).then_inc(shift_ready, 1)
                apart(dve, passed)
                for t in range(NT):
                    ins = dve.max_index(top_at[:, t, :], top[:, t, :], ps_logits[:, t, :])
                step(ins)
                yield
                settle()
                step(dve.tensor_tensor(pick[:], expert_f[:].unsqueeze(1).unsqueeze(2).broadcast_to([P, NT, 2, E]),
                                       top_at[:, :, 0:2].unsqueeze(3).broadcast_to([P, NT, 2, E]), ALU.is_equal))
                yield
                settle()
                dve.tensor_tensor(both16[:], pick[:, :, 0, :], pick[:, :, 1, :], ALU.add).then_inc(both_ready, 1)

            def combine_weights(r, par):
                after(dve, expl_ready, r.value(1, 1))
                done = 0

                def step(ins):
                    nonlocal done
                    ins.then_inc(route_w, 1)
                    done += 1

                step(dve.tensor_reduce(prob_sum[:], expl[:], AX.X, ALU.add))
                yield
                after(dve, route_w, r.value(3, done))
                step(dve.reciprocal(prob_inv[:], prob_sum[:]))
                yield
                after(dve, route_w, r.value(3, done))
                after(dve, both_ready, r.value(1, 1))
                step(dve.tensor_tensor(weight[:], both16[:], wide(prob_inv[:]), ALU.mult))
                yield
                after(dve, route_w, r.value(3, done))
                after(dve, row_ready, r.value(2, 2))
                dve.tensor_tensor(rows[:, par, :, D:D + E], weight[:], expl[:], ALU.mult).then_inc(cw_ready, 1)

            def take_slots(r, par):
                after(dve, ranks_made, r.value(1, 1))
                done = 0

                def step(ins):
                    nonlocal done
                    ins.then_inc(route_s, 1)
                    done += 1

                def settle():
                    after(dve, route_s, r.value(4, done))

                step(dve.tensor_tensor(slot[:], ps_rank_pair, next_row[:].unsqueeze(1).broadcast_to([P, NT, E]), ALU.add))
                yield
                settle()
                step(dve.tensor_tensor(next_row[:], ps_ranks[NT], next_row[:], ALU.add))
                yield
                settle()
                step(dve.tensor_tensor(slot_of[:], pick[:], slot[:].unsqueeze(2).broadcast_to([P, NT, 2, E]), ALU.mult))
                yield
                settle()
                step(dve.tensor_reduce(slot_f[:], slot_of[:], AX.X, ALU.add))
                yield
                settle()
                dve.tensor_copy(slot_u[:, par, :, :], slot_f[:]).then_inc(slots_ready, 1)

            def low_weights(e, parity, n):
                cols = slice(n * PIECE, (n + 1) * PIECE)
                dve.wait_ge(e_hi_ready, e * PIECES + (n + 1))
                dve.scalar_tensor_tensor(e_lo[:, parity, cols], e_stage[:, cols], WS, e_hi[:, parity, cols],
                                         ALU.mult, ALU.subtract).then_inc(e_lo_ready, 1)

            def low_early(pieces):
                for n in pieces:
                    low_weights(0, 0, n)

            def body(n, a, b, c, r, z):
                m = n or (c and c + 3)
                under_way = []

                def between():
                    for chain in under_way:
                        next(chain, None)

                def finish(chain):
                    for _ in chain:
                        pass

                def start(chain):
                    under_way.append(chain)

                weights_chain = combine_weights(z, z.plus % 2) if z else None
                slots_chain = take_slots(z, z.plus % 2) if z else None
                inner = {2: [(a, low_x)],
                         3: [(n, lambda j: sum_x(j, 0, xin, x_in, 16, x_summed)),
                             (r, lambda j: high_rows(j, j.plus % 2))],
                         4: [(c, residual)]}
                outer = {0: [(a, full_kv)],
                         1: [(c, lambda j: normalize(j, 1))],
                         2: [(c, low_att)],
                         4: [(c, lambda j: sum_x(j, 1, x2, x2_ready, 1, x2_summed)), (a, lambda j: low_q(j, j.plus % 2)),
                             (m, lambda j: start(statistics(j, n, c)))],
                         5: [(b, lambda j: normalize(j, 0))],
                         6: [(z, lambda j: finish(weights_chain)), (z, lambda j: finish(slots_chain)),
                             (early_pieces(c, r), low_early)]}
                starts = {1: [(z, lambda j: start(weights_chain))],
                          2: [(z, lambda j: start(slots_chain))],
                          7: [(r, lambda j: start(route_top(j)))]}
                for u in range(UNITS):
                    for at, stage in starts.get(u, []):
                        if at:
                            stage(at)
                    following = unit(c, b, a, u + 1)
                    if following:
                        maximum(*following)
                        between()
                    if (at := unit(c, b, a, u - 1)) and at[1] not in LOW_ON_ACT:
                        low_probs(*at)
                        between()
                    for at, stage in inner.get(u, []):
                        if at:
                            stage(at)
                            between()
                    if following:
                        shift(*following)
                        between()
                    for at, stage in outer.get(u, []):
                        if at:
                            stage(at)
                            between()
                while under_way:
                    under_way = [chain for chain in under_way if next(chain, False) is None]

            batches(dve, body)

            dve.wait_ge(slots_ready, B)
            done = 0

            def step(ins):
                nonlocal done
                ins.then_inc(counted, 1)
                done += 1
                dve.wait_ge(counted, done)

            step(dve.tensor_copy(count_f[:], region_i[0:1, :]))
            step(dve.tensor_tensor(count_f[:], next_row[0:1, :], count_f[:], ALU.subtract))
            step(dve.tensor_scalar(tiles_f[:], count_f[:], float(TS - 1), 1.0 / TS, ALU.add, ALU.mult))
            step(dve.tensor_scalar(tiles_f[:], tiles_f[:], (TS - 1) / (2.0 * TS), 2.0, ALU.subtract, ALU.max))
            dve.tensor_copy(tiles_i[:], tiles_f[:]).then_inc(tables_ready, 1)
            dve.tensor_copy(pad_i[:], next_row[0:1, :]).then_inc(tables_ready, 1)
            dve.wait_ge(tables_ready, 2)
            step(dve.tensor_copy(tiles_g[:], tiles_i[:]))
            step(dve.memset(base_a[:], 0.0))
            step(dve.tensor_copy(base_a[:, 1:E], tiles_g[:, 0:E - 1]))
            src, dst = base_a, base_b
            for by in (1, 2, 4):
                step(dve.tensor_copy(dst[:, 0:by], src[:, 0:by]))
                step(dve.tensor_tensor(dst[:, by:E], src[:, by:E], src[:, 0:E - by], ALU.add))
                src, dst = dst, src
            dve.tensor_copy(base_i[:], src[:]).then_inc(tables_ready, 1)
            step(dve.tensor_scalar(rest_f[:], tiles_g[:], -1.0, None, ALU.add))
            dve.tensor_copy(rest_i[:], rest_f[:]).then_inc(tables_ready, 1)
            step(dve.scalar_tensor_tensor(spare_f[:], tiles_g[:], float(TS), count_f[:], ALU.mult, ALU.subtract))
            step(dve.tensor_scalar(half_f[:], spare_f[:], float(TS - P), None, ALU.is_ge))
            dve.tensor_copy(half_i[:], half_f[:]).then_inc(tables_ready, 1)
            dve.wait_ge(tables_ready, 5)

            dve.memset(w_row[:], 0.0).then_inc(raw_free, 1)
            dve.memset(y_sb[:], 0.0).then_inc(y_ready, 1)
            low_early(range(EARLY, PIECES))

            def h_step(g, s):
                if s == STEPS - 1:
                    dve.wait_ge(gu_made, g * STEPS + STEPS)
                    dve.wait_ge(xg_turned, g + 2)
                    dve.tensor_copy(xg[:, 1, :, :], ps_xt[1]).then_inc(xg_vec, 1)
                dve.wait_ge(silu_ready, g * STEPS + (s + 1))
                dve.scalar_tensor_tensor(h_full[:, s % 2, :], ps_up[s % 2][:], H_DOWN, g_act[:, s % 2, :],
                                         ALU.mult, ALU.mult).then_inc(h_ready, 1)
                dve.wait_ge(h_hi_ready, g * STEPS + (s + 1))
                dve.tensor_tensor(h_lo[:, 2 * s:2 * s + 2, :].rearrange("p f t -> p (f t)"), h_full[:, s % 2, :],
                                  h_hi[:, 2 * s:2 * s + 2, :].rearrange("p f t -> p (f t)"), ALU.subtract).then_inc(h_lo_ready, 1)

            def take_rows(g):
                dve.tensor_copy(tail_in[:], raw[:, :, D:RW]).then_inc(raw_free, 1)

            dve.wait_ge(xg_turned, 1)
            dve.tensor_copy(xg[:, 1, :, :], ps_xt[1]).then_inc(xg_vec, 1)
            take_rows(0)
            h_step(0, 0)

            def tile(g, e, parity, prepare):
                for n, s in enumerate((1, 2, 3, 0)):
                    h_step(g if s else g + 1, s)
                    if s == STEPS - 1:
                        dve.wait_ge(added, g * 32 + 16)
                        dve.wait_ge(raw_free, g + 2)
                        dve.tensor_copy(tok_row[:], tail_in[:, :, E].bitcast(U32)).then_inc(meta_ready, 1)
                        dve.tensor_copy(w_row[:], tail_in[:, :, bass.ds(e, 1)].rearrange("p s w -> p (s w)")).then_inc(meta_ready, 1)
                        dve.wait_ge(meta_ready, g * 2 + 2)
                        take_rows(g + 1)
                    if s == 0:
                        dve.wait_ge(y_made, g + 1)
                        for half in range(2):
                            dve.tensor_scalar(y_sb[:, half, :], ps_y[half][:, 0:D], w_row[:, half:half + 1], 8.0 / WS,
                                              ALU.mult, ALU.mult).then_inc(y_ready, 1)
                    if prepare:
                        for piece in range(PIECES_AT[n], PIECES_AT[n + 1]):
                            low_weights(e + 1, 1 - parity, piece)

            def tiles(e, parity, first, n):
                tile(first, e, parity, True)
                with dve.Fori(1, n) as j:
                    tile(dve.snap(first + j), e, parity, False)

            experts(dve, tiles)

        @block.gpsimd
        def _(pool):
            pool.memset(ident[:], 0.0).then_inc(const_base, 1)
            pool.memset(ident16[:], 0.0).then_inc(const_base, 1)
            pool.memset(minus16[:], 0.0).then_inc(const_base, 1)
            pool.memset(before[:], 1.0).then_inc(const_base, 1)
            pool.memset(head_mask[:], 1.0).then_inc(const_base, 1)
            pool.memset(pads[:], 0.0).then_inc(const_base, 1)
            pool.wait_ge(const_base, 6)
            pool.affine_select(out=ident[:], in_=ident[:], compare_op=ALU.not_equal, fill=1.0, base=0,
                               pattern=[[-1, P]], channel_multiplier=1).then_inc(const_ready, 1)
            pool.affine_select(out=ident16[:], in_=ident16[:], compare_op=ALU.not_equal, fill=1.0, base=0,
                               pattern=[[-1, P]], channel_multiplier=1).then_inc(const_ready, 1)
            pool.affine_select(out=minus16[:], in_=minus16[:], compare_op=ALU.not_equal, fill=-1.0, base=0,
                               pattern=[[-1, P]], channel_multiplier=1).then_inc(const_ready, 1)
            pool.affine_select(out=before[:], in_=before[:], compare_op=ALU.is_ge, fill=0.0, base=-1,
                               pattern=[[1, P]], channel_multiplier=-1).then_inc(const_ready, 1)
            pool.affine_select(out=head_mask[:], in_=head_mask[:], compare_op=ALU.is_ge, fill=0.0, base=0,
                               pattern=[[-DK, P // DK]], channel_multiplier=1).then_inc(const_base, 1)
            pool.wait_ge(const_base, 7)
            pool.affine_select(out=head_mask[:], in_=head_mask[:], compare_op=ALU.is_ge, fill=0.0, base=DK - 1,
                               pattern=[[DK, P // DK]], channel_multiplier=-1).then_inc(const_ready, 1)
            pool.memset(ones16[:], 1.0).then_inc(const_ready, 1)
            pool.iota(expert_i[:], pattern=[[1, E]], base=0, channel_multiplier=0).then_inc(const_ready, 1)
            pool.iota(region_i[:], pattern=[[REGION, E]], base=0, channel_multiplier=0).then_inc(const_ready, 1)
            pool.iota(token_i[:], pattern=[[P, NT]], base=0, channel_multiplier=1).then_inc(const_ready, 1)
            pool.iota(pads[:, :, RW - 1].bitcast(I32), pattern=[[P, 2]], base=T, channel_multiplier=1).then_inc(const_ready, 1)
            for par in range(2):
                pool.memset(v_parts[:, par, 0, :, DK:VW], 1.0).then_inc(ones_set, 1)
                pool.memset(v_parts[:, par, 1, :, DK:VW], 0.0).then_inc(ones_set, 1)
            pool.wait_ge(const_ready, 10)
            pool.wait_ge(ones_set, 4)
            pool.dma_start(out[T:T + TS, :].rearrange("(s p) d -> p s d", p=P), pads[:, :, 0:D]).then_inc(added, 16)

            def split_cx(j):
                after(pool, cx_in, j.value(16, 16))
                after(pool, kv_made, j.value(1))
                apart(pool, passed)
                pool.tensor_copy(cx_hi[:], cx[:]).then_inc(cx_hi_ready, 1)
                after(pool, cx_hi_ready, j.value(1, 1))
                pool.tensor_tensor(cx_lo[:], cx[:], cx_hi[:], ALU.subtract).then_inc(cx_lo_ready, 1)

            def split_kv(j, par):
                after(pool, kv_full, j.value(KC + 1, KC + 1))
                after(pool, kd_ready, j.value(1))
                apart(pool, passed)
                pool.tensor_copy(k_parts[:, 0, :, :], k_full[:]).then_inc(k_part, 1)
                after(pool, pv_made, j.value(UNITS, -UNITS))
                v_heads = v_full[:].rearrange("k (h w) -> k h w", h=H)
                apart(pool, passed)
                pool.tensor_copy(v_parts[:, par, 0, :, 0:DK], v_heads).then_inc(v_part, 1)
                after(pool, k_part, j.value(2, 1))
                pool.tensor_tensor(k_parts[:, 1, :, :], k_full[:], k_parts[:, 0, :, :], ALU.subtract).then_inc(k_part, 1)
                after(pool, v_part, j.value(2, 1))
                pool.tensor_tensor(v_parts[:, par, 1, :, 0:DK], v_heads, v_parts[:, par, 0, :, 0:DK], ALU.subtract).then_inc(v_part, 1)

            def spread_keys(j, par):
                after(pool, k_part, j.value(2, 2))
                heads = P // DK
                pool.tensor_tensor(k_diag[:, par].rearrange("p l c h k -> p (l c) h k"),
                                   k_parts[:].rearrange("p l c k -> p (l c) k").unsqueeze(2).broadcast_to([P, 2 * KC, heads, KS]),
                                   head_mask[:].unsqueeze(1).unsqueeze(3).broadcast_to([P, 2 * KC, heads, KS]),
                                   ALU.mult).then_inc(kd_ready, 1)

            def add_bias(j):
                after(pool, xres_in, j.value(16, 16))
                pool.tensor_tensor(xres[:], xres[:], bo[:].unsqueeze(1).broadcast_to([P, NT, D]), ALU.add).then_inc(xb_ready, 1)

            def make_rows(j, par):
                after(pool, scattered, j.value(SCATTER, -SCATTER))
                parts = rows[:, par, :, 0:D].bitcast(F16)
                apart(pool, passed)
                pool.tensor_copy(rows[:, par, :, RW - 1].bitcast(I32), token_i[:]).then_inc(row_ready, 1)
                after(pool, row_hi_ready, j.value(1, 1))
                after(pool, row_ready, j.value(2, 1))
                pool.tensor_tensor(parts[:, :, D:2 * D], x2n[:], parts[:, :, 0:D], ALU.subtract).then_inc(row_ready, 1)
                pool.tensor_scalar(token_i[:], token_i[:], float(S), None, ALU.add).then_inc(token_ready, 1)
                after(pool, token_ready, j.value(1, 1))

            def scatter(r, par):
                after(pool, row_ready, r.value(2, 2))
                after(pool, cw_ready, r.value(1, 1))
                after(pool, slots_ready, r.value(1, 1))
                apart(pool, passed)
                for t in range(NT):
                    for k in range(2):
                        pool.indirect_dma_start(rows_dram, bass.IndirectOffsetOnAxis(slot_u[:, par, t, k:k + 1], 0),
                                                rows[:, par, t, :], None).then_inc(scattered, 16)

            def body(n, a, b, c, r, z):
                if a:
                    split_kv(a, a.plus % 2)
                if a:
                    spread_keys(a, a.plus % 2)
                if r:
                    make_rows(r, r.plus % 2)
                if n:
                    split_cx(n)
                if z:
                    scatter(z, z.plus % 2)
                if b:
                    add_bias(b)

            pool.wait_ge(r_in, 80)
            batches(pool, body)

            pool.wait_ge(x2_out, 16 * B)
            pool.wait_ge(tables_ready, 5)

            def tiles(e, parity, first, n):
                with pool.Fori(0, n) as j:
                    g = pool.snap(first + j)
                    pool.wait_ge(added, g * 32 + 16)
                    pool.wait_ge(meta_ready, g * 2 + 2)
                    for half in range(2):
                        pool.wait_ge(y_ready, g * 2 + (half + 2))
                        apart(pool, passed)
                        pool.indirect_dma_start(out, bass.IndirectOffsetOnAxis(tok_row[:, half:half + 1], 0),
                                                y_sb[:, half, :], None, compute_op=ALU.add).then_inc(added, 16)

            experts(pool, tiles)


def kernel(**inputs):
    import concourse.bacc as bacc
    from concourse.bass_utils import run_bass_kernel_spmd

    g = {n: np.asarray(a) for n, a in inputs.items()}
    turned = lambda a: np.ascontiguousarray(np.swapaxes(a, -1, -2))
    columns = lambda a: a.reshape(KC, P).T
    arrays = {
        "x": np.ascontiguousarray(g["x"].reshape(T, D)),
        "ctx_t": turned(g["ctx_1024"]),
        "w_q": turned(g["L0_xattn_w_q"]), "b_q": columns(g["L0_xattn_b_q"]),
        "w_k": turned(g["L0_xattn_w_k"]), "b_k": columns(g["L0_xattn_b_k"]),
        "w_v": turned(g["L0_xattn_w_v"]), "b_v": g["L0_xattn_b_v"],
        "w_o": turned(g["L0_xattn_w_o"]), "b_o": g["L0_xattn_b_o"],
        "router_w": g["L0_ffn_router_w"], "gate_w": g["L0_ffn_gate_w"],
        "up_w": g["L0_ffn_up_w"], "down_w": g["L0_ffn_down_w"],
    }
    nc = bacc.Bacc("TRN2", target_bir_lowering=False, num_devices=1)
    arrays = {f"in_{n}": np.ascontiguousarray(a) for n, a in arrays.items()}
    args = [nc.dram_tensor(n, a.shape, mybir.dt.from_np(a.dtype), kind="ExternalInput").ap() for n, a in arrays.items()]
    args.append(nc.dram_tensor("out_0", (T + TS, D), F32, kind="ExternalOutput").ap())
    build(nc, *args)
    result = run_bass_kernel_spmd(nc, [arrays], core_ids=[0])
    return result.results[0]["out_0"][0:T].reshape(B, S, D)
```
